# Optimizing a Trainium2 kernel written in Bass

```python
import numpy as np
import jax
import jax.numpy as jnp

def _softmax(x, axis=-1):
    return jax.nn.softmax(x, axis=axis)

def _gelu(x):
    return jax.nn.gelu(x, approximate=True)

def _silu(x):
    return jax.nn.silu(x)

def _sigmoid(x):
    return jax.nn.sigmoid(x)

def _layernorm(x, axis=-1, eps=1e-05):
    m = jnp.mean(x, axis=axis, keepdims=True)
    v = jnp.var(x, axis=axis, keepdims=True)
    return (x - m) / jnp.sqrt(v + eps)

def _scatter_add(tgt, idx, src, axis=0):
    return tgt.at[idx].add(src)

def _segment_sum(src, seg, n):
    return jax.ops.segment_sum(src, seg, n)
kernel_name = 'mk_audio_tower_d1_tok_audfeat256_r4_5776eb'

def setup_inputs(seed: int=0):
    np.random.seed(seed)
    _w = jnp.asarray

    def _rec_inputs():
        import jax
        import jax.numpy as jnp
        _rk = jax.random.key(seed)
        x = -0.000392918 + 0.999932 * jax.random.normal(jax.random.fold_in(_rk, 1), (8, 750, 64), jnp.float32)
        return x
    x = _rec_inputs()

    def _L0_tok_setup():
        import jax, jax.numpy as jnp
        import numpy as np
        from jax import lax
        B, S, CIN, COUT, K = (32, 512, 64, 64, 16)
        key = jax.random.key(seed)
        k1, k2, k3, k4 = jax.random.split(key, 4)
        x = jax.random.normal(k1, (B, S, CIN), dtype=jnp.float32)
        w_real = jax.random.normal(k2, (COUT, CIN, K), dtype=jnp.float32) * 0.1
        w_imag = jax.random.normal(k3, (COUT, CIN, K), dtype=jnp.float32) * 0.1
        phases = jax.random.normal(k4, (K,), dtype=jnp.float32) * 0.1
        return {'x': x, 'w_real': w_real, 'w_imag': w_imag, 'phases': phases}
    _L0_tok_all = _L0_tok_setup()
    _L0_tok_in = {k: v for k, v in _L0_tok_all.items() if k in ('w_real', 'w_imag', 'phases')}
    del _L0_tok_all

    def _L0_attn_setup():
        import jax, jax.numpy as jnp
        import numpy as np
        B, S, I, H, O = (64, 128, 64, 256, 64)

        def _rnn_layer(inp, W_ih, W_hh, b_ih, b_hh):
            pre = jnp.einsum('bsi,hi->bsh', inp, W_ih) + (b_ih + b_hh)
            h0 = jnp.zeros((inp.shape[0], W_hh.shape[0]), dtype=inp.dtype)

            def step(h, p_t):
                h = jnp.tanh(p_t + h @ W_hh.T)
                return (h, h)
            _, hs = jax.lax.scan(step, h0, jnp.swapaxes(pre, 0, 1))
            return jnp.swapaxes(hs, 0, 1)
        key = jax.random.key(seed)
        ks = jax.random.split(key, 12)
        s_in = 1.0 / np.sqrt(H)
        inp = {'x': jax.random.normal(ks[0], (B, S, I), dtype=jnp.float32), 'W_ih_0': jax.random.uniform(ks[1], (H, I), jnp.float32, -s_in, s_in), 'W_hh_0': jax.random.uniform(ks[2], (H, H), jnp.float32, -s_in, s_in), 'b_ih_0': jax.random.uniform(ks[3], (H,), jnp.float32, -s_in, s_in), 'b_hh_0': jax.random.uniform(ks[4], (H,), jnp.float32, -s_in, s_in), 'W_ih_1': jax.random.uniform(ks[5], (H, H), jnp.float32, -s_in, s_in), 'W_hh_1': jax.random.uniform(ks[6], (H, H), jnp.float32, -s_in, s_in), 'b_ih_1': jax.random.uniform(ks[7], (H,), jnp.float32, -s_in, s_in), 'b_hh_1': jax.random.uniform(ks[8], (H,), jnp.float32, -s_in, s_in), 'fc_w': jax.random.uniform(ks[9], (O, H), jnp.float32, -s_in, s_in), 'fc_b': jax.random.uniform(ks[10], (O,), jnp.float32, -s_in, s_in)}
        return inp
    _L0_attn_all = _L0_attn_setup()
    _L0_attn_in = {k: v for k, v in _L0_attn_all.items() if k in ('W_ih_0', 'W_hh_0', 'b_ih_0', 'b_hh_0', 'W_ih_1', 'W_hh_1', 'b_ih_1', 'b_hh_1', 'fc_w', 'fc_b')}
    del _L0_attn_all

    def _L0_ffn_setup():
        import jax, jax.numpy as jnp
        import numpy as np
        INPUT_WIDTH = 64
        DEPTH = 7
        OUTPUT_WIDTH = 64
        N_NODES = 2 ** (DEPTH + 1) - 1
        key = jax.random.key(seed)
        k_x, k_w1, k_w2 = jax.random.split(key, 3)
        init1 = 1.0 / np.sqrt(INPUT_WIDTH)
        x = jax.random.normal(k_x, (2, 256, INPUT_WIDTH), dtype=jnp.float32)
        w1s = jax.random.uniform(k_w1, (N_NODES, INPUT_WIDTH), jnp.float32, -init1, init1)
        b1s = jnp.zeros((N_NODES,), jnp.float32)
        w2s = jax.random.uniform(k_w2, (N_NODES, INPUT_WIDTH, OUTPUT_WIDTH), jnp.float32, -init1, init1)
        b2s = jnp.zeros((N_NODES, OUTPUT_WIDTH), jnp.float32)
        return {'x': x, 'w1s': w1s, 'b1s': b1s, 'w2s': w2s, 'b2s': b2s}
    _L0_ffn_all = _L0_ffn_setup()
    _L0_ffn_in = {k: v for k, v in _L0_ffn_all.items() if k in ('w1s', 'b1s', 'w2s', 'b2s')}
    del _L0_ffn_all
    return {'x': x, 'L0_tok_w_real': _L0_tok_in['w_real'], 'L0_tok_w_imag': _L0_tok_in['w_imag'], 'L0_tok_phases': _L0_tok_in['phases'], 'L0_attn_W_ih_0': _L0_attn_in['W_ih_0'], 'L0_attn_W_hh_0': _L0_attn_in['W_hh_0'], 'L0_attn_b_ih_0': _L0_attn_in['b_ih_0'], 'L0_attn_b_hh_0': _L0_attn_in['b_hh_0'], 'L0_attn_W_ih_1': _L0_attn_in['W_ih_1'], 'L0_attn_W_hh_1': _L0_attn_in['W_hh_1'], 'L0_attn_b_ih_1': _L0_attn_in['b_ih_1'], 'L0_attn_b_hh_1': _L0_attn_in['b_hh_1'], 'L0_attn_fc_w': _L0_attn_in['fc_w'], 'L0_attn_fc_b': _L0_attn_in['fc_b'], 'L0_ffn_w1s': _L0_ffn_in['w1s'], 'L0_ffn_b1s': _L0_ffn_in['b1s'], 'L0_ffn_w2s': _L0_ffn_in['w2s'], 'L0_ffn_b2s': _L0_ffn_in['b2s']}

def reference(x, L0_tok_w_real, L0_tok_w_imag, L0_tok_phases, L0_attn_W_ih_0, L0_attn_W_hh_0, L0_attn_b_ih_0, L0_attn_b_hh_0, L0_attn_W_ih_1, L0_attn_W_hh_1, L0_attn_b_ih_1, L0_attn_b_hh_1, L0_attn_fc_w, L0_attn_fc_b, L0_ffn_w1s, L0_ffn_b1s, L0_ffn_w2s, L0_ffn_b2s):
    import jax
    import jax.numpy as jnp

    def _L0_tok_ref(x, w_real, w_imag, phases):
        import jax, jax.numpy as jnp
        import numpy as np
        from jax import lax
        B, S, CIN, COUT, K = (32, 512, 64, 64, 16)
        w_eff = jnp.cos(phases)[None, None, :] * w_real - jnp.sin(phases)[None, None, :] * w_imag
        y = lax.conv_general_dilated(jnp.transpose(x, (0, 2, 1)), w_eff, window_strides=(1,), padding='VALID', dimension_numbers=('NCH', 'OIH', 'NCH'))
        return jnp.transpose(y, (0, 2, 1))

    def _L0_attn_ref(x, W_ih_0, W_hh_0, b_ih_0, b_hh_0, W_ih_1, W_hh_1, b_ih_1, b_hh_1, fc_w, fc_b):
        import jax, jax.numpy as jnp
        import numpy as np
        B, S, I, H, O = (64, 128, 64, 256, 64)

        def _rnn_layer(inp, W_ih, W_hh, b_ih, b_hh):
            pre = jnp.einsum('bsi,hi->bsh', inp, W_ih) + (b_ih + b_hh)
            h0 = jnp.zeros((inp.shape[0], W_hh.shape[0]), dtype=inp.dtype)

            def step(h, p_t):
                h = jnp.tanh(p_t + h @ W_hh.T)
                return (h, h)
            _, hs = jax.lax.scan(step, h0, jnp.swapaxes(pre, 0, 1))
            return jnp.swapaxes(hs, 0, 1)
        h = _rnn_layer(x, W_ih_0, W_hh_0, b_ih_0, b_hh_0)
        h = _rnn_layer(h, W_ih_1, W_hh_1, b_ih_1, b_hh_1)
        return h @ fc_w.T + fc_b

    def _L0_ffn_ref(x, w1s, b1s, w2s, b2s):
        import jax, jax.numpy as jnp
        import numpy as np
        INPUT_WIDTH = 64
        DEPTH = 7
        OUTPUT_WIDTH = 64
        N_NODES = 2 ** (DEPTH + 1) - 1
        B, S, D = x.shape
        flat_x = x.reshape(B * S, D)
        T = flat_x.shape[0]
        current = jnp.zeros((T,), dtype=jnp.int32)
        all_nodes = []
        all_logits = []
        for _ in range(DEPTH + 1):
            all_nodes.append(current)
            score = jnp.einsum('td,td->t', flat_x, w1s[current]) + b1s[current]
            all_logits.append(score)
            choice = ((jnp.sign(score) + 1.0) / 2.0).astype(jnp.int32)
            current = current * 2 + choice + 1
        logits = jnp.stack(all_logits, axis=1)
        path_weights = jax.nn.gelu(jnp.abs(logits), approximate=False)
        out = jnp.zeros((T, OUTPUT_WIDTH), dtype=x.dtype)
        for i in range(DEPTH + 1):
            nodes_i = all_nodes[i]
            t_i = jnp.einsum('td,tdo->to', flat_x, w2s[nodes_i]) + b2s[nodes_i]
            out = out + t_i * path_weights[:, i][:, None]
        return out.reshape(B, S, OUTPUT_WIDTH)
    h = _L0_tok_ref(x, L0_tok_w_real, L0_tok_w_imag, L0_tok_phases)
    h = h + _L0_attn_ref(_layernorm(h, axis=-1), L0_attn_W_ih_0, L0_attn_W_hh_0, L0_attn_b_ih_0, L0_attn_b_hh_0, L0_attn_W_ih_1, L0_attn_W_hh_1, L0_attn_b_ih_1, L0_attn_b_hh_1, L0_attn_fc_w, L0_attn_fc_b)
    h = h + _L0_ffn_ref(_layernorm(h, axis=-1), L0_ffn_w1s, L0_ffn_b1s, L0_ffn_w2s, L0_ffn_b2s)
    return h

_drawn_inputs = setup_inputs


def setup_inputs(seed=0):
    import zlib

    import numpy as np

    out = dict(_drawn_inputs(seed))
    spreads = {'L0_ffn_b1s': (0.0, 0.1), 'L0_ffn_b2s': (0.0, 0.1)}
    factors = {'L0_attn_b_ih_0': 3.379, 'L0_attn_b_hh_0': 3.369}
    for name, (base, spread) in spreads.items():
        noise = np.random.default_rng([zlib.crc32(name.encode()), seed]).standard_normal(out[name].shape)
        drawn = base * np.exp(spread * noise) if base else spread * noise
        out[name] = jnp.asarray(drawn.astype(out[name].dtype))
    for name, factor in factors.items():
        out[name] = (out[name] * factor).astype(out[name].dtype)
    return out
```

```python
import concourse.bass as bass
from concourse import mybir
from contextlib import ExitStack

F32 = mybir.dt.float32
F16 = mybir.dt.float16
BF16 = mybir.dt.bfloat16
I32 = mybir.dt.int32
ALU = mybir.AluOpType
ACT = mybir.ActivationFunctionType
AX = mybir.AxisListType

P = 128
B, SIN, CH, K = 8, 750, 64, 16
S = SIN - K + 1
NT = B * S
H = 256
KH, MH = H // P, H // P
C = 15
NCH = S // C
TT = C * B
CONVN = 490
NCONV = NT // CONVN
LEVELS = 8
NODES = 2 ** LEVELS - 1
LEAVES = 2 ** (LEVELS - 1)
WROWS = CH + 1
WCOLS = LEVELS * CH
NWIN = (NT + LEAVES * (P - 1)) // P
NSLOT = NWIN * P
ROW = CH + LEVELS
WSCALE = 256.0
EPS = 1e-5
PI = 3.141592653589793
TWO_PI_HIGH = 6.28125
TWO_PI_LOW = 2 * PI - TWO_PI_HIGH
ROUND = 1.5 * 2 ** 23

PREP_LINKS = 18
N_TABLE_DMAS = sum(1 + min(2 ** l, LEAVES >> l) for l in range(LEVELS))
N_POOL_SETUP = 26

assert NCH * C == S and NCONV * CONVN == NT


def stages(c):
    return c < NCH, 0 <= c - 2 < NCH, 0 <= c - 3 < NCH, 0 <= c - 1 < NCH, c + 1 < NCH


def run_chunks(eng, chunk):
    for c in range(3):
        chunk(c, c % 2, stages(c))
    pairs = (NCH - 1 - 3) // 2
    with eng.Fori(0, pairs) as j:
        chunk(3 + 2 * j, 1, (True,) * 5)
        chunk(4 + 2 * j, 0, (True,) * 5)
    for c in range(3 + 2 * pairs, NCH + 3):
        chunk(c, c % 2, stages(c))


def tower(nc, xT, w_real, w_imag, phases, wih0, whh0, bih0, bhh0, wih1, whh1, bih1, bhh1,
          fcw, fcb, w1, b1, w2, b2, out):
    w_leaf = nc.dram_tensor("w_leaf", (LEAVES * WROWS, WCOLS), F32, kind="Internal").ap()
    sorted_in = nc.dram_tensor("sorted_in", (NSLOT, ROW), F32, kind="Internal").ap()
    sorted_out = nc.dram_tensor("sorted_out", (NSLOT, CH), F32, kind="Internal").ap()

    with ExitStack() as ctx:
        def sb(name, shape, dt=F32):
            return ctx.enter_context(nc.sbuf_tensor(name, shape, dt))

        def sem(name):
            return ctx.enter_context(nc.semaphore(name))

        x2 = sb("x2", [P, SIN * B])
        wr = sb("wr", [P, K // 2, CH])
        wi = sb("wi", [P, K // 2, CH])
        ph = sb("ph", [P, K // 2])
        trig = sb("trig", [P, 2, K // 2])
        turns = sb("turns", [P, 2, K // 2])
        wc = sb("wc", [P, K // 2, 2, CH])
        wtmp = sb("wtmp", [P, K // 2, CH])
        w_f32 = sb("w_f32", [P, 4, 2 * H])
        fc_f32 = sb("fc_f32", [P, KH, CH])
        bias_f32 = sb("bias_f32", [1, 4, H])
        fcb_f32 = sb("fcb_f32", [1, CH])
        wih0_p = sb("wih0_p", [P, 2, H], F16)
        whh0_p = sb("whh0_p", [P, 2, KH * H], F16)
        wih1_p = sb("wih1_p", [P, 2, KH * H], F16)
        whh1_p = sb("whh1_p", [P, 2, KH * H], F16)
        fc_p = sb("fc_p", [P, 2, KH * CH], F16)
        bias_s = sb("bias_s", [1, 2, H])
        bias_p = sb("bias_p", [1, 2, 2, H], F16)
        fcb_p = sb("fcb_p", [1, 2, CH], F16)
        ones_row = sb("ones_row", [1, P], F16)
        w1_sb = sb("w1_sb", [WROWS, NODES])
        ident = sb("ident", [P, P])
        ident_s = sb("ident_s", [CH, CH])
        mean_w = sb("mean_w", [CH, P])
        before = sb("before", [TT, P], BF16)
        ones_bf = sb("ones_bf", [TT, P], BF16)
        ones_f = sb("ones_f", [P, P])
        leaf_no = sb("leaf_no", [P, LEAVES])
        win_no = sb("win_no", [P, NWIN])
        part_no = sb("part_no", [P, 1])
        eps_t = sb("eps_t", [P, 1])
        mhalf = sb("mhalf", [P, CONVN])
        zero_row = sb("zero_row", [P, ROW])
        first_p = sb("first_p", [P, 1])
        hconv = sb("hconv", [CH, NT])
        dev = sb("dev", [P, 2, CONVN])
        sq = sb("sq", [P, 2, CONVN])
        rstd = sb("rstd", [P, 2, CONVN])
        x1s = sb("x1s", [P, NT], F16)
        h_hi = [sb(f"h{l}_hi", [P, 2, KH, TT], F16) for l in range(2)]
        h_lo = [sb(f"h{l}_lo", [P, 2, KH, TT], F16) for l in range(2)]
        h_f = [sb(f"h{l}_f", [P, KH, B]) for l in range(2)]
        hct = sb("hct", [CH, 2, TT])
        h2 = sb("h2", [TT, NCH, CH])
        st = sb("st", [TT, 6])
        mv = sb("mv", [TT, 2])
        rs2 = sb("rs2", [TT, 1])
        xrow = sb("xrow", [TT, NCH, ROW])
        xn_t = sb("xn_t", [TT, ROW])
        d2 = sb("d2", [TT, CH])
        xnT = sb("xnT", [WROWS, TT])
        sc = sb("sc", [TT, NODES])
        right = sb("right", [TT, LEAVES - 1])
        mask = sb("mask", [TT, NODES])
        msc = sb("msc", [TT, NODES])
        rkr = sb("rkr", [TT, LEAVES])
        plog = sb("plog", [TT, LEVELS])
        mask_bf = sb("mask_bf", [TT, NCH, LEAVES], BF16)
        rk = sb("rk", [P, 2, LEAVES])
        rkm = sb("rkm", [TT, LEAVES])
        rank_t = sb("rank_t", [TT, 1])
        rank = sb("rank", [TT, NCH])
        cnt = sb("cnt", [P, LEAVES])
        cnt_i = sb("cnt_i", [P, LEAVES], I32)
        wins = sb("wins", [P, LEAVES])
        cums = sb("cums", [P, 2, LEAVES])
        base = sb("base", [P, LEAVES])
        cumT = sb("cumT", [P, 1])
        past = sb("past", [P, NWIN])
        widx_f = sb("widx_f", [P, NWIN])
        widx = sb("widx", [P, NWIN], I32)
        posm = sb("posm", [TT, 7, LEAVES])
        posb = sb("posb", [TT, NCH])
        pos = sb("pos", [TT, NCH], I32)
        NB = 4
        widx_w = [sb(f"widx_w{i}", [WROWS, 1], I32) for i in range(NB)]
        xs = [sb(f"xs{i}", [P, ROW]) for i in range(NB)]
        wl = [sb(f"wl{i}", [WROWS, WCOLS]) for i in range(NB)]
        xsT = [sb(f"xsT{i}", [WROWS, P]) for i in range(NB)]
        prod = [sb(f"prod{i}", [P, WCOLS]) for i in range(2)]
        os_ = [sb(f"os{i}", [P, CH]) for i in range(NB)]
        back = sb("back", [TT, NCH, CH])

        banks = [ctx.enter_context(nc.psum_tensor(f"bank{i}", [P, 512], F32)) for i in range(8)]
        pre = [[banks[0], banks[1]], [banks[2], banks[3]]]
        p_fc, p_tr, p_sc, p_rk = banks[4], banks[5], banks[6], banks[7]
        p_conv = [banks[0], banks[1]]
        p_mean = [banks[2], banks[3]]
        p_var = [banks[4], banks[5]]
        p_xT = [banks[0], banks[1]]
        p_y = [banks[2], banks[3]]

        (s_x, s_xb, s_wc, s_wt, s_wload, s_w1load, s_pool, s_trig, s_sin, s_wconv, s_split, s_zero, s_leafw,
         s_conv, s_meand, s_hcopy, s_dev, s_sqd, s_vard, s_vare, s_rst, s_x1,
         s_hct, s_h2, s_fc) = [sem(n) for n in (
            "x_first_half x_second_half wconv_loaded wt w_loaded w1_loaded pool_setup trig_ready sin_done wconv_ready split_done "
            "zero_filled leafw_filled conv_done mean_done hconv_copied dev_ready squares_ready "
            "var_done var_eps_ready rstd_ready x1_ready hct_ready h2_ready fc_done").split()]
        s_mm = [sem(f"rec{l}_done") for l in range(2)]
        s_hi = [sem(f"h{l}_high_ready") for l in range(2)]
        s_lo = [sem(f"h{l}_low_ready") for l in range(2)]
        s_stat, s_mask, s_rkm, s_rank, s_xn, s_xrow, s_xnT, s_xnTc, s_sc, s_scc, s_m7, s_rk, s_rkc, s_plog, s_pw, s_pchain = [sem(n) for n in (
            "stats_ready all_masks_ready rkm_ready rank_ready xn_ready xrow_ready xnT_done xnT_copied scores_done scores_copied mask_ready rank_done rank_copied "
            "plog_ready pw_ready pool_step").split()]
        s_bn, s_lev, s_rankt, s_dchain, s_cum, s_cumT, s_past, s_leafp, s_widx, s_widxw, s_pos = [sem(n) for n in (
            "bn_ready level_scores rank_t_ready dve_step cum_ready cumT_done past_ready winleaf_done widx_ready window_widx_ready pos_ready").split()]
        s_passed = sem("passed")
        s_scat = sem("rows_scattered")
        s_xs = [sem(f"xs{i}_loaded") for i in range(NB)]
        s_wl = [sem(f"wl{i}_loaded") for i in range(NB)]
        s_out5 = [sem(f"os{i}_stored") for i in range(NB)]
        s_xt, s_xtc, s_y, s_prod, s_o = [sem(n) for n in "xsT_done xsT_copied y_done prod_done o_ready".split()]
        s_back, s_sum, s_fin = sem("rows_back"), sem("sum_ready"), sem("out_stored")

        block = ctx.enter_context(nc.Block())

        @block.sync
        def _(sp):
            sp.dma_start(ph[0:CH, :], phases[0:1, :].broadcast_to([CH, K // 2])).then_inc(s_wc, 16)
            sp.dma_start(ph[CH:P, :], phases[1:2, :].broadcast_to([CH, K // 2])).then_inc(s_wc, 16)
            sp.dma_start(wr[:, :, :], w_real).then_inc(s_wc, 16)
            sp.dma_start(wi[:, :, :], w_imag).then_inc(s_wc, 16)
            half = (SIN * B) // 2
            sp.dma_start(x2[0:CH, 0:half], xT[:, 0:half]).then_inc(s_x, 16)
            sp.dma_start(x2[CH:P, 0:half], xT[:, B:half + B]).then_inc(s_x, 16)
            sp.dma_start(x2[0:CH, half:], xT[:, half:]).then_inc(s_xb, 16)
            sp.dma_start(x2[CH:P, half:SIN * B - B], xT[:, half + B:]).then_inc(s_xb, 16)
            sp.dma_start(w_f32[0:CH, 0, 0:H], wih0).then_inc(s_wload, 16)
            sp.dma_start(w_f32[CH:P, 0, 0:H], wih0).then_inc(s_wload, 16)
            for n, w in ((1, whh0), (2, wih1), (3, whh1)):
                sp.dma_start(w_f32[:, n, :].rearrange("p (k h) -> p k h", k=KH),
                             w.rearrange("(k p) h -> p k h", p=P)).then_inc(s_wload, 16)
            sp.dma_start(fc_f32[:, :, :], fcw.rearrange("(k p) h -> p k h", p=P)).then_inc(s_wload, 16)
            for n, b in enumerate((bih0, bhh0, bih1, bhh1)):
                sp.dma_start(bias_f32[0:1, n, :], b).then_inc(s_wload, 16)
            sp.dma_start(fcb_f32[0:1, :], fcb).then_inc(s_wload, 16)
            sp.dma_start(w1_sb[0:CH, :], w1).then_inc(s_w1load, 16)
            sp.dma_start(w1_sb[CH:WROWS, :], b1).then_inc(s_w1load, 16)
            table = w_leaf.rearrange("(f r) c -> f r c", r=WROWS)
            for l in range(LEVELS):
                n0, n, rep = 2 ** l - 1, 2 ** l, LEAVES >> l
                cols = slice(l * CH, (l + 1) * CH)
                if n < rep:
                    for m in range(n):
                        sp.dma_start(table[m * rep:(m + 1) * rep, 0:CH, cols],
                                     w2[n0 + m:n0 + m + 1, :, :].broadcast_to([rep, CH, CH])).then_inc(s_leafw, 16)
                else:
                    for m in range(rep):
                        sp.dma_start(table[m::rep, 0:CH, cols], w2[n0:n0 + n, :, :]).then_inc(s_leafw, 16)
                sp.dma_start(table[:, CH, cols].rearrange("(n r) c -> n r c", r=rep),
                             b2[n0:n0 + n, :].unsqueeze(1).broadcast_to([n, rep, CH])).then_inc(s_leafw, 16)
            sp.wait_ge(s_pool, N_POOL_SETUP)
            sp.dma_start(sorted_in.rearrange("(w p) c -> p w c", p=P),
                         zero_row[:, :].unsqueeze(1).broadcast_to([P, NWIN, ROW])).then_inc(s_zero, 16)
            sp.wait_ge(s_scat, 16 * NCH)

            def window(w, i, first):
                if not first:
                    sp.wait_ge(s_o, w - NB + 1)
                    sp.wait_ge(s_xt, w - NB + 1)
                sp.dma_start(xs[i][:, :], sorted_in[bass.ds(w * P, P), :]).then_inc(s_xs[i], 16)

            for i in range(NB):
                window(i, i, True)
            with sp.Fori(1, NWIN // NB) as j:
                for i in range(NB):
                    window(j * NB + i, i, False)
            sp.wait_ge(s_sum, 1)
            sp.dma_start(out.rearrange("(i p) c -> p i c", p=TT), back[:, :, :]).then_inc(s_fin, 16)
            sp.wait_ge(s_fin, 16)

        @block.gpsimd
        def _(pool):
            done = [0]

            def setup(ins):
                done[0] += 1
                ins.then_inc(s_pool, 1)
                pool.wait_ge(s_pool, done[0])

            setup(pool.memset(ones_f[:, :], 1.0))
            setup(pool.memset(ident[:, :], 0.0))
            setup(pool.memset(ident_s[:, :], 0.0))
            setup(pool.memset(mean_w[:, :], 1.0 / CH))
            setup(pool.memset(before[:, :], 0.0))
            setup(pool.memset(ones_bf[:, :], 1.0))
            setup(pool.memset(eps_t[:, :], EPS))
            setup(pool.memset(mhalf[:, :], -0.5))
            setup(pool.memset(zero_row[:, :], 0.0))
            setup(pool.memset(first_p[:, :], 0.0))
            setup(pool.memset(ones_row[:, :], 1.0))
            setup(pool.memset(cnt[:, :], 0.0))
            setup(pool.memset(mask[:, 0:1], 1.0))
            setup(pool.memset(xn_t[:, :], 0.0))
            setup(pool.memset(xnT[CH:WROWS, :], 1.0))
            for i in range(NB):
                setup(pool.memset(xsT[i][CH:WROWS, :], 1.0))
            setup(pool.iota(leaf_no[:, :], pattern=[[1, LEAVES]], base=0, channel_multiplier=0,
                            allow_small_or_imprecise_dtypes=True))
            setup(pool.iota(win_no[:, :], pattern=[[1, NWIN]], base=0, channel_multiplier=0,
                            allow_small_or_imprecise_dtypes=True))
            setup(pool.iota(part_no[:, :], pattern=[[1, 1]], base=0, channel_multiplier=1,
                            allow_small_or_imprecise_dtypes=True))
            setup(pool.affine_select(out=ident[:, :], in_=ident[:, :], compare_op=ALU.not_equal, fill=1.0,
                                     base=0, pattern=[[-1, P]], channel_multiplier=1))
            setup(pool.affine_select(out=ident_s[:, :], in_=ident_s[:, :], compare_op=ALU.not_equal,
                                     fill=WSCALE, base=0, pattern=[[-1, CH]], channel_multiplier=1))
            setup(pool.affine_select(out=before[:, :], in_=before[:, :], compare_op=ALU.is_ge, fill=1.0,
                                     base=0, pattern=[[-1, P]], channel_multiplier=1))
            setup(pool.affine_select(out=first_p[:, :], in_=first_p[:, :], compare_op=ALU.not_equal, fill=1.0,
                                     base=0, pattern=[[-1, 1]], channel_multiplier=1))
            for i in range(NCONV):
                pool.wait_ge(s_vare, i + 1)
                pool.tensor_tensor(rstd[:, i % 2, :], rstd[:, i % 2, :], mhalf[:, :], ALU.pow).then_inc(s_rst, 1)

            pool.wait_ge(s_hcopy, NCONV)

            def residual(t, q, first):
                if not first:
                    pool.wait_ge(s_fc, t - 1)
                pool.tensor_copy(hct[:, q, :], hconv[:, bass.ds(t * TT, TT)]).then_inc(s_hct, 1)

            residual(0, 0, True)
            residual(1, 1, True)
            with pool.Fori(1, NCH // 2) as j:
                residual(2 * j, 0, False)
                residual(2 * j + 1, 1, False)
            residual(NCH - 1, 0, False)

            def prep(i):
                step = [0]

                def link(ins):
                    step[0] += 1
                    ins.then_inc(s_pchain, 1)
                    pool.wait_ge(s_pchain, i * PREP_LINKS + step[0])

                x = h2[:, bass.ds(i, 1), :].rearrange("p a c -> p (a c)")
                pool.wait_ge(s_stat, i + 1)
                link(pool.tensor_tensor(rs2[:, :], mv[:, 1:2], eps_t[0:TT, :], ALU.add))
                link(pool.tensor_tensor(rs2[:, :], rs2[:, :], mhalf[0:TT, 0:1], ALU.pow))
                link(pool.tensor_tensor(d2[:, :], x, mv[:, 0:1].broadcast_to([TT, CH]), ALU.subtract))
                pool.tensor_tensor(xn_t[:, 0:CH], d2[:, :], rs2[:, :].broadcast_to([TT, CH]),
                                   ALU.mult).then_inc(s_xn, 1)
                pool.wait_ge(s_xn, i + 1)
                pool.tensor_copy(xrow[:, bass.ds(i, 1), 0:CH].rearrange("p a c -> p (a c)"),
                                 xn_t[:, 0:CH]).then_inc(s_xrow, 1)
                pool.wait_ge(s_scc, i + 1)
                pool.sem_inc(s_passed, 1)
                link(pool.tensor_scalar(right[:, :], sc[:, 0:LEAVES - 1], 0.0, None, ALU.is_gt))
                for l in range(LEVELS - 1):
                    a, n = 2 ** l - 1, 2 ** l
                    kids = mask[:, 2 * n - 1:4 * n - 1].rearrange("p (n t) -> p n t", t=2)
                    link(pool.tensor_tensor(kids[:, :, 1], mask[:, a:a + n], right[:, a:a + n], ALU.mult))
                    last = pool.tensor_tensor(kids[:, :, 0], mask[:, a:a + n], kids[:, :, 1], ALU.subtract)
                    if l < LEVELS - 2:
                        link(last)
                last.then_inc(s_mask, 1)
                pool.wait_ge(s_mask, i + 1)
                pool.tensor_copy(mask_bf[:, bass.ds(i, 1), :].rearrange("p a c -> p (a c)"),
                                 mask[:, LEAVES - 1:NODES]).then_inc(s_m7, 1)
                pool.wait_ge(s_rkc, i + 1)
                pool.tensor_tensor(rkm[:, :], rk[0:TT, 0, :], cnt[0:TT, :], ALU.add).then_inc(s_rkm, 1)
                pool.wait_ge(s_rkm, i + 1)
                link(pool.tensor_tensor(cnt[:, :], cnt[:, :], rk[:, 1, :], ALU.add))
                pool.wait_ge(s_rank, i + 1)
                assert step[0] == PREP_LINKS, step[0]

            with pool.Fori(0, NCH) as i:
                prep(i)

            pool.wait_ge(s_zero, 16)
            pool.wait_ge(s_pw, NCH)
            pool.wait_ge(s_xrow, NCH)
            pool.wait_ge(s_pos, 1)
            for i in range(NCH):
                pool.indirect_dma_start(sorted_in, bass.IndirectOffsetOnAxis(ap=pos[:, i:i + 1], axis=0),
                                        xrow[:, i, :], None).then_inc(s_scat, 16)
            pool.wait_ge(s_leafw, 16 * N_TABLE_DMAS)
            pool.wait_ge(s_widx, 1)

            def window(w, i, first):
                if not first:
                    pool.wait_ge(s_wl[i], w * (16 // NB) - i * (16 // NB))
                pool.tensor_copy(widx_w[i][:, :], widx[0:WROWS, bass.ds(w, 1)]).then_inc(s_widxw, 1)
                pool.wait_ge(s_widxw, w + 1)
                if not first:
                    pool.wait_ge(s_y, w - NB + 1)
                pool.sem_inc(s_passed, 1)
                pool.indirect_dma_start(wl[i][:, :], None, w_leaf,
                                        bass.IndirectOffsetOnAxis(ap=widx_w[i][:, 0:1], axis=0)
                                        ).then_inc(s_wl[i], 16)

            for i in range(NB):
                window(i, i, True)
            with pool.Fori(1, NWIN // NB) as j:
                for i in range(NB):
                    window(j * NB + i, i, False)
            for i in range(NB):
                pool.wait_ge(s_out5[i], 16 * (NWIN // NB))
            for i in range(NCH):
                pool.indirect_dma_start(back[:, i, :], None, sorted_out,
                                        bass.IndirectOffsetOnAxis(ap=pos[:, i:i + 1], axis=0)).then_inc(s_back, 16)

        @block.vector
        def _(dve):
            v = nc.vector
            chain = [0]

            def link(ins):
                chain[0] += 1
                ins.then_inc(s_dchain, 1)
                dve.wait_ge(s_dchain, chain[0])

            dve.wait_ge(s_wc, 64)
            link(v.tensor_scalar(trig[:, 0, :], ph[:, :], PI / 2, None, ALU.add))
            link(v.tensor_copy(trig[:, 1, :], ph[:, :]))
            link(v.tensor_scalar(turns[:, :, :], trig[:, :, :], 1 / (2 * PI), ROUND, ALU.mult, ALU.add))
            link(v.tensor_scalar(turns[:, :, :], turns[:, :, :], ROUND, None, ALU.subtract))
            link(v.scalar_tensor_tensor(trig[:, :, :], turns[:, :, :], -TWO_PI_HIGH, trig[:, :, :],
                                        ALU.mult, ALU.add))
            link(v.scalar_tensor_tensor(trig[:, :, :], turns[:, :, :], -TWO_PI_LOW, trig[:, :, :],
                                        ALU.mult, ALU.add))
            v.tensor_scalar(trig[:, :, :], trig[:, :, :], 3.1415925, -3.1415925, ALU.min, ALU.max).then_inc(s_trig, 1)
            dve.wait_ge(s_sin, 1)
            for k in range(K // 2):
                link(v.tensor_scalar(wtmp[:, k, :], wi[:, k, :], trig[:, 1, k:k + 1], None, ALU.mult))
                for half in range(2):
                    v.scalar_tensor_tensor(wc[:, k, half, :], wr[:, k, :], trig[:, 0, k:k + 1], wtmp[:, k, :],
                                           ALU.mult, ALU.subtract).then_inc(s_wconv, 1)
            dve.wait_ge(s_wload, 16 * 11)
            link(v.tensor_tensor(bias_s[0:1, 0, :], bias_f32[0:1, 0, :], bias_f32[0:1, 1, :], ALU.add))
            link(v.tensor_tensor(bias_s[0:1, 1, :], bias_f32[0:1, 2, :], bias_f32[0:1, 3, :], ALU.add))
            for part, full in ((wih0_p, w_f32[:, 0, 0:H]), (whh0_p, w_f32[:, 1, :]), (wih1_p, w_f32[:, 2, :]),
                               (whh1_p, w_f32[:, 3, :]), (fc_p, fc_f32[:, :, :].rearrange("p k c -> p (k c)")), (fcb_p, fcb_f32[0:1, :]),
                               (bias_p[:, :, :, :].rearrange("p a l h -> p a (l h)"),
                                bias_s[:, :, :].rearrange("p l h -> p (l h)"))):
                link(v.tensor_scalar(part[:, 0, :], full, WSCALE, None, ALU.mult))
                link(v.scalar_tensor_tensor(part[:, 1, :], full, WSCALE, part[:, 0, :], ALU.mult, ALU.subtract))
            v.memset(turns[:, :, :], 0.0).then_inc(s_split, 1)
            for i in range(NCONV):
                j, tok = i % 2, slice(i * CONVN, (i + 1) * CONVN)
                dve.wait_ge(s_meand, i + 1)
                if i >= 2:
                    dve.wait_ge(s_x1, i - 1)
                v.tensor_tensor(dev[:, j, :], sq[:, j, :], p_mean[j][:, 0:CONVN], ALU.subtract).then_inc(s_dev, 1)
                dve.wait_ge(s_vard, i + 1)
                v.tensor_scalar(rstd[:, j, :], p_var[j][:, 0:CONVN], EPS, None, ALU.add).then_inc(s_vare, 1)
                dve.wait_ge(s_rst, i + 1)
                link(v.tensor_tensor(dev[:, j, :], dev[:, j, :], rstd[:, j, :], ALU.mult))
                link(v.tensor_copy(x1s[:, tok], dev[:, j, :]))
                v.tensor_tensor(x1s[CH:P, tok], dev[CH:P, j, :], x1s[CH:P, tok], ALU.subtract).then_inc(s_x1, 1)

            def low(l, c, k, q):
                dve.wait_ge(s_hi[l], c * C + k + 1)
                col = slice(k * B, (k + 1) * B)
                v.tensor_tensor(h_lo[l][:, q, :, col], h_f[l][:, :, :], h_hi[l][:, q, :, col],
                                ALU.subtract).then_inc(s_lo[l], 1)

            def chunk(c, q, on):
                for k in range(C):
                    if on[0]:
                        low(0, c, k, q)
                    if on[1]:
                        low(1, c - 2, k, q)

            run_chunks(dve, chunk)

            def prep(i):
                dve.wait_ge(s_h2, i + 1)
                x = h2[:, bass.ds(i, 1), :].rearrange("p a c -> p (a c)")
                v.bn_stats(st[:, :], x).then_inc(s_bn, 1)
                dve.wait_ge(s_bn, i + 1)
                dve.sem_inc(s_passed, 1)
                v.bn_aggr(mv[:, :], st[:, :]).then_inc(s_stat, 1)
                dve.wait_ge(s_mask, i + 1)
                for l in range(LEVELS):
                    nodes = slice(2 ** l - 1, 2 ** (l + 1) - 1)
                    v.tensor_tensor_reduce(out=msc[:, nodes], in0=mask[:, nodes], in1=sc[:, nodes], scale=1.0,
                                           scalar=0.0, op0=ALU.mult, op1=ALU.add,
                                           accum_out=plog[:, l:l + 1]).then_inc(s_lev, 1)
                dve.wait_ge(s_lev, i * LEVELS + LEVELS)
                v.scalar_tensor_tensor(plog[:, :], plog[:, :], -1.0, plog[:, :], ALU.mult, ALU.max).then_inc(s_plog, 1)
                dve.wait_ge(s_rkm, i + 1)
                v.tensor_tensor_reduce(out=rkr[:, :], in0=rkm[:, :], in1=mask[:, LEAVES - 1:NODES], scale=1.0,
                                       scalar=0.0, op0=ALU.mult, op1=ALU.add,
                                       accum_out=rank_t[:, :]).then_inc(s_rankt, 1)
                dve.wait_ge(s_rankt, i + 1)
                v.tensor_tensor(rank[:, bass.ds(i, 1)], rank_t[:, :], rank_t[:, :], ALU.max).then_inc(s_rank, 1)

            with dve.Fori(0, NCH) as i:
                prep(i)

            dve.wait_ge(s_pchain, NCH * PREP_LINKS)
            link(v.tensor_scalar(wins[:, :], cnt[:, :], float(P - 1), None, ALU.add))
            link(v.tensor_copy(cnt_i[:, :], wins[:, :]))
            link(v.tensor_scalar(cnt_i[:, :], cnt_i[:, :], 7, None, ALU.arith_shift_right))
            link(v.tensor_copy(wins[:, :], cnt_i[:, :]))
            link(v.tensor_copy(cums[:, 0, :], wins[:, :]))
            a, d = 0, 1
            while d < LEAVES:
                link(v.tensor_copy(cums[:, 1 - a, 0:d], cums[:, a, 0:d]))
                link(v.tensor_tensor(cums[:, 1 - a, d:], cums[:, a, d:], cums[:, a, 0:LEAVES - d], ALU.add))
                a, d = 1 - a, 2 * d
            link(v.tensor_tensor(base[:, :], cums[:, a, :], wins[:, :], ALU.subtract))
            link(v.tensor_scalar(base[:, :], base[:, :], float(P), None, ALU.mult))
            if a != 1:
                link(v.tensor_copy(cums[:, 1, :], cums[:, 0, :]))
            v.memset(cnt_i[:, :], 0).then_inc(s_cum, 1)
            dve.wait_ge(s_cumT, 1)
            link(v.tensor_copy(cumT[:, :], p_tr[:, 0:1]))
            v.tensor_scalar(past[:, :], win_no[:, :], cumT[:, 0:1], None, ALU.is_ge).then_inc(s_past, 1)
            dve.wait_ge(s_leafp, 1)
            link(v.tensor_scalar(widx_f[:, :], p_sc[:, 0:NWIN], float(LEAVES - 1), float(WROWS), ALU.min, ALU.mult))
            v.tensor_scalar(widx[:, :], widx_f[:, :], part_no[:, 0:1], None, ALU.add).then_inc(s_widx, 1)
            for g in range(NCH // 7):
                tiles = slice(7 * g, 7 * g + 7)
                link(v.tensor_tensor(posm[:, :, :], mask_bf[:, tiles, :],
                                     base[0:TT, :].unsqueeze(1).broadcast_to([TT, 7, LEAVES]), ALU.mult))
                link(v.tensor_reduce(posb[:, tiles], posm[:, :, :], AX.X, ALU.add))
            v.tensor_tensor(pos[:, :], posb[:, :], rank[:, :], ALU.add).then_inc(s_pos, 1)

            def window(w, i, first):
                dve.wait_ge(s_y, w + 1)
                dve.wait_ge(s_xs[i], w * (16 // NB) + 16 - i * (16 // NB))
                if not first:
                    dve.wait_ge(s_o, w - 1)
                v.tensor_tensor(prod[i % 2][:, :].rearrange("p (l o) -> p l o", l=LEVELS),
                                p_y[i % 2][:, :].rearrange("p (l o) -> p l o", l=LEVELS),
                                xs[i][:, CH:ROW].unsqueeze(2).broadcast_to([P, LEVELS, CH]),
                                ALU.mult).then_inc(s_prod, 1)
                dve.wait_ge(s_prod, w + 1)
                if not first:
                    dve.wait_ge(s_out5[i], w * (16 // NB) - i * (16 // NB))
                v.tensor_reduce(os_[i][:, :], prod[i % 2][:, :].rearrange("p (l o) -> p o l", l=LEVELS),
                                AX.X, ALU.add).then_inc(s_o, 1)

            for i in range(NB):
                window(i, i, True)
            with dve.Fori(1, NWIN // NB) as j:
                for i in range(NB):
                    window(j * NB + i, i, False)
            dve.wait_ge(s_back, 16 * NCH)
            v.tensor_tensor(back[:, :, :], back[:, :, :], h2[:, :, :], ALU.add).then_inc(s_sum, 1)

        @block.scalar
        def _(act):
            a = nc.scalar
            act.wait_ge(s_trig, 1)
            a.activation(trig[:, :, :], trig[:, :, :], ACT.Sin).then_inc(s_sin, 1)
            a.preload_act_table_set("gelu_and_others")
            for i in range(NCONV):
                j, tok = i % 2, slice(i * CONVN, (i + 1) * CONVN)
                act.wait_ge(s_conv, i + 1)
                a.activation(hconv[:, tok], p_conv[j][0:CH, 0:CONVN], ACT.Copy)
                if i >= 2:
                    act.wait_ge(s_vard, i - 1)
                a.activation(sq[:, j, :], p_conv[j][:, 0:CONVN], ACT.Copy).then_inc(s_hcopy, 1)
                act.wait_ge(s_dev, i + 1)
                a.activation(sq[:, j, :], dev[:, j, :], ACT.Square).then_inc(s_sqd, 1)

            def tanh(l, c, k, q):
                act.wait_ge(s_mm[l], c * C + k + 1)
                col = slice(k * B, (k + 1) * B)
                z = pre[l][q][:, 0:MH * TT].rearrange("p (m n) -> p m n", m=MH)[:, :, col]
                a.activation(h_f[l][:, :, :], z, ACT.Tanh, scale=1 / WSCALE)
                a.activation(h_hi[l][:, q, :, col], z, ACT.Tanh, scale=1 / WSCALE).then_inc(s_hi[l], 1)

            def chunk(c, q, on):
                for k in range(C):
                    if on[0]:
                        tanh(0, c, k, q)
                    if on[1]:
                        tanh(1, c - 2, k, q)
                if on[2]:
                    t = c - 3
                    act.wait_ge(s_fc, t + 1)
                    a.activation(h2[:, bass.ds(t, 1), :].rearrange("p a c -> p (a c)"), p_fc[0:TT, 0:CH],
                                 ACT.Copy, scale=1 / WSCALE).then_inc(s_h2, 1)

            run_chunks(act, chunk)

            with act.Fori(0, NCH) as i:
                act.wait_ge(s_xnT, i + 1)
                a.activation(xnT[0:CH, :], p_tr[0:CH, 0:TT], ACT.Copy).then_inc(s_xnTc, 1)
                act.wait_ge(s_sc, i + 1)
                a.activation(sc[:, :], p_sc[0:TT, 0:NODES], ACT.Copy).then_inc(s_scc, 1)
                act.wait_ge(s_rk, i + 1)
                a.activation(rk[:, :, :].rearrange("p a c -> p (a c)"), p_rk[:, 0:2 * LEAVES],
                             ACT.Copy).then_inc(s_rkc, 1)
                act.wait_ge(s_plog, i + 1)
                a.activation(xrow[:, bass.ds(i, 1), CH:ROW].rearrange("p a c -> p (a c)"), plog[:, :],
                             ACT.Gelu).then_inc(s_pw, 1)

            def window(w, i, first):
                act.wait_ge(s_xt, w + 1)
                if not first:
                    act.wait_ge(s_y, w - NB + 1)
                a.activation(xsT[i][0:CH, :], p_xT[i % 2][0:CH, 0:P], ACT.Copy).then_inc(s_xtc, 1)

            def store(w, i):
                act.wait_ge(s_o, w + 1)
                act.dma_start(sorted_out[bass.ds(w * P, P), :], os_[i][:, :]).then_inc(s_out5[i], 16)

            for i in range(NB):
                window(i, i, True)
            with act.Fori(1, NWIN // NB) as j:
                for i in range(NB):
                    window(j * NB + i, i, False)
                    store((j - 1) * NB + i, i)
            for i in range(NB):
                store(NWIN - NB + i, i)

        @block.tensor
        def _(pe):
            mm = nc.tensor.matmul
            pe.wait_ge(s_wconv, K)
            pe.wait_ge(s_pool, N_POOL_SETUP)

            def conv(i):
                pe.wait_ge(s_x, 32)
                if (i + 1) * CONVN + (K - 1) * B > SIN * B // 2:
                    pe.wait_ge(s_xb, 32)
                if i >= 2:
                    pe.wait_ge(s_hcopy, i - 1)
                for k in range(K // 2):
                    at = i * CONVN + 2 * k * B
                    last = mm(p_conv[i % 2][:, 0:CONVN], wc[:, k, :, :].rearrange("p a c -> p (a c)"),
                              x2[:, at:at + CONVN], start=(k == 0), stop=(k == K // 2 - 1))
                last.then_inc(s_conv, 1)

            def stats(i):
                j = i % 2
                pe.wait_ge(s_hcopy, i + 1)
                if i >= 2:
                    pe.wait_ge(s_dev, i - 1)
                mm(p_mean[j][:, 0:CONVN], mean_w[:, :], sq[0:CH, j, :], start=True, stop=True).then_inc(s_meand, 1)
                pe.wait_ge(s_sqd, i + 1)
                if i >= 2:
                    pe.wait_ge(s_vare, i - 1)
                mm(p_var[j][:, 0:CONVN], mean_w[:, :], sq[0:CH, j, :], start=True, stop=True).then_inc(s_vard, 1)

            conv(0)
            for i in range(NCONV):
                if i + 1 < NCONV:
                    conv(i + 1)
                stats(i)

            def shared(z, w, x, start=False):
                return mm(z, w, x, start=start, stop=True, skip_group_check=True)

            def bias(z, row, last_inc=None):
                shared(z, row(0), ones_row[0:1, 0:TT])
                last = shared(z, row(1), ones_row[0:1, 0:TT])
                if last_inc is not None:
                    last.then_inc(last_inc, 1)

            def pre0(n, q, piece):
                m, j = divmod(piece, 3)
                z, ms = pre[0][q][:, m * TT:(m + 1) * TT], slice(m * P, (m + 1) * P)
                if j < 2:
                    shared(z, wih0_p[:, j, ms], x1s[:, bass.ds(n * TT, TT)], start=(piece == 0))
                else:
                    first = m == MH - 1 and isinstance(n, int) and n == 0
                    bias(z, lambda p: bias_p[0:1, p, 0, ms], s_mm[0] if first else None)

            def pre1(n, q, piece):
                m, j = divmod(piece, 7)
                z, ms = pre[1][q][:, m * TT:(m + 1) * TT], slice(m * P, (m + 1) * P)
                if j < 6:
                    k, (p, h) = j // 3, ((0, h_hi), (0, h_lo), (1, h_hi))[j % 3]
                    shared(z, wih1_p[:, p, k * H + m * P:k * H + (m + 1) * P], h[0][:, q, k, :],
                           start=(piece == 0))
                else:
                    first = m == MH - 1 and isinstance(n, int) and n == 0
                    bias(z, lambda p: bias_p[0:1, p, 1, ms], s_mm[1] if first else None)

            def fc(t, q, piece):
                z = p_fc[0:TT, 0:CH]
                if piece == 0 and not (isinstance(t, int) and t == 0):
                    pe.wait_ge(s_h2, t)
                if piece < 6:
                    k, (p, h) = piece // 3, ((0, h_hi), (0, h_lo), (1, h_hi))[piece % 3]
                    mm(z, h[1][:, q, k, :], fc_p[:, p, k * CH:(k + 1) * CH], start=(piece == 0), stop=False)
                elif piece == 6:
                    for p in range(2):
                        mm(z, ones_row[0:1, 0:TT], fcb_p[0:1, p, :], start=False, stop=False)
                else:
                    pe.wait_ge(s_hct, t + 1)
                    mm(z, hct[:, q, :], ident_s[:, :], start=False, stop=True).then_inc(s_fc, 1)

            def side(n, c, q, on):
                if n < 6:
                    if on[4]:
                        pre0(c + 1, 1 - q, n)
                elif n < 20:
                    if on[3]:
                        pre1(c - 1, 1 - q, n - 6)
                elif n < 28:
                    if on[2]:
                        fc(c - 3, 1 - q, n - 20)

            def recur(l, c, k, q):
                if k == 0 and isinstance(c, int) and c == 0:
                    return
                w = (whh0_p, whh1_p)[l]
                pq, pk = (q, k - 1) if k else (1 - q, C - 1)
                cols = slice(pk * B, (pk + 1) * B)
                z = [pre[l][q][:, m * TT + k * B:m * TT + (k + 1) * B] for m in range(MH)]
                pe.wait_ge(s_hi[l], c * C + k)
                for p in range(2):
                    for m in range(MH):
                        for kk in range(KH):
                            shared(z[m], w[:, p, kk * H + m * P:kk * H + (m + 1) * P], h_hi[l][:, pq, kk, cols])
                pe.wait_ge(s_lo[l], c * C + k)
                for m in range(MH):
                    for kk in range(KH):
                        last = shared(z[m], w[:, 0, kk * H + m * P:kk * H + (m + 1) * P],
                                      h_lo[l][:, pq, kk, cols])
                last.then_inc(s_mm[l], 1)

            def chunk(c, q, on):
                if on[3] and not on[0]:
                    pe.wait_ge(s_hi[0], S)
                    pe.wait_ge(s_lo[0], S)
                if on[2] and not on[1]:
                    pe.wait_ge(s_hi[1], S)
                    pe.wait_ge(s_lo[1], S)
                for k in range(C):
                    if on[0]:
                        recur(0, c, k, q)
                    if k:
                        side(2 * k - 1, c, q, on)
                    if on[1]:
                        recur(1, c - 2, k, q)
                    side(2 * k, c, q, on)

            pe.wait_ge(s_split, 1)
            pe.wait_ge(s_x1, NCONV)
            for piece in range(6):
                pre0(0, 0, piece)
            run_chunks(pe, chunk)

            pe.wait_ge(s_w1load, 32)
            with pe.Fori(0, NCH) as i:
                pe.wait_ge(s_xn, i + 1)
                nc.tensor.transpose(p_tr[0:ROW, 0:TT], xn_t[:, :], ident[0:TT, 0:TT]).then_inc(s_xnT, 1)
                pe.wait_ge(s_xnTc, i + 1)
                mm(p_sc[0:TT, 0:NODES], xnT[:, :], w1_sb[:, :], start=True, stop=True).then_inc(s_sc, 1)
                pe.wait_ge(s_m7, i + 1)
                m7 = mask_bf[:, bass.ds(i, 1), :].rearrange("p a c -> p (a c)")
                mm(p_rk[:, 0:LEAVES], before[:, :], m7, start=True, stop=False)
                mm(p_rk[:, LEAVES:2 * LEAVES], ones_bf[:, :], m7, start=False, stop=True).then_inc(s_rk, 1)

            pe.wait_ge(s_cum, 1)
            mm(p_tr[:, 0:1], cums[:, 1, :], first_p[:, :], start=True, stop=True).then_inc(s_cumT, 1)
            pe.wait_ge(s_past, 1)
            mm(p_sc[:, 0:NWIN], ones_f[:, :], past[:, :], start=True, stop=True).then_inc(s_leafp, 1)

            def turn(j, i, first):
                w = j * NB + i
                pe.wait_ge(s_xs[i], j * 16 + 16)
                if not (first and i < 2):
                    pe.wait_ge(s_xtc, w - 1)
                nc.tensor.transpose(p_xT[i % 2][0:ROW, 0:P], xs[i][:, :], ident[:, :]).then_inc(s_xt, 1)

            def path(j, i, first):
                w = j * NB + i
                pe.wait_ge(s_xtc, w + 1)
                pe.wait_ge(s_wl[i], j * 16 + 16)
                if not (first and i < 2):
                    pe.wait_ge(s_prod, w - 1)
                mm(p_y[i % 2][:, :], xsT[i][:, :], wl[i][:, :], start=True, stop=True).then_inc(s_y, 1)

            def windows(j, first, last=False):
                for i in range(NB):
                    if i + 1 < NB:
                        turn(j, i + 1, first)
                    elif not last:
                        turn(j + 1, 0, False)
                    path(j, i, first)

            turn(0, 0, True)
            windows(0, True)
            with pe.Fori(1, NWIN // NB - 1) as j:
                windows(j, False)
            windows(NWIN // NB - 1, False, last=True)


def kernel(x, L0_tok_w_real, L0_tok_w_imag, L0_tok_phases, L0_attn_W_ih_0, L0_attn_W_hh_0,
           L0_attn_b_ih_0, L0_attn_b_hh_0, L0_attn_W_ih_1, L0_attn_W_hh_1, L0_attn_b_ih_1,
           L0_attn_b_hh_1, L0_attn_fc_w, L0_attn_fc_b, L0_ffn_w1s, L0_ffn_b1s, L0_ffn_w2s, L0_ffn_b2s):
    import numpy as np
    import concourse.bacc as bacc
    from concourse.bass_utils import run_bass_kernel_spmd

    def taps(w):
        return np.asarray(w).transpose(2, 1, 0).reshape(K // 2, 2, CH, CH).transpose(1, 2, 0, 3).reshape(P, K // 2, CH)

    laid_out = {
        "xT": np.asarray(x).transpose(2, 1, 0).reshape(CH, SIN * B),
        "w_real": taps(L0_tok_w_real),
        "w_imag": taps(L0_tok_w_imag),
        "phases": np.asarray(L0_tok_phases).reshape(K // 2, 2).T,
        "wih0": np.asarray(L0_attn_W_ih_0).T,
        "whh0": np.asarray(L0_attn_W_hh_0).T,
        "bih0": np.asarray(L0_attn_b_ih_0).reshape(1, H),
        "bhh0": np.asarray(L0_attn_b_hh_0).reshape(1, H),
        "wih1": np.asarray(L0_attn_W_ih_1).T,
        "whh1": np.asarray(L0_attn_W_hh_1).T,
        "bih1": np.asarray(L0_attn_b_ih_1).reshape(1, H),
        "bhh1": np.asarray(L0_attn_b_hh_1).reshape(1, H),
        "fcw": np.asarray(L0_attn_fc_w).T,
        "fcb": np.asarray(L0_attn_fc_b).reshape(1, CH),
        "w1": np.asarray(L0_ffn_w1s).T,
        "b1": np.asarray(L0_ffn_b1s).reshape(1, NODES),
        "w2": np.asarray(L0_ffn_w2s),
        "b2": np.asarray(L0_ffn_b2s),
    }
    nc = bacc.Bacc("TRN2", target_bir_lowering=False, num_devices=1)
    arrays, args = {}, []
    for name, a in laid_out.items():
        a = np.ascontiguousarray(a)
        arrays[name + "_dram"] = a
        args.append(nc.dram_tensor(name + "_dram", a.shape, mybir.dt.from_np(a.dtype), kind="ExternalInput").ap())
    args.append(nc.dram_tensor("out_dram", (NT, CH), F32, kind="ExternalOutput").ap())
    tower(nc, *args)
    r = run_bass_kernel_spmd(nc, [arrays], core_ids=[0])
    got = r.results[0]["out_dram"]
    return got.reshape(S, B, CH).transpose(1, 0, 2)
```

```python
import concourse.bass as bass
from concourse import mybir
from contextlib import ExitStack

F32 = mybir.dt.float32
F16 = mybir.dt.float16
BF16 = mybir.dt.bfloat16
I32 = mybir.dt.int32
ALU = mybir.AluOpType
ACT = mybir.ActivationFunctionType
AX = mybir.AxisListType

P = 128
B, SIN, CH, K = 8, 750, 64, 16
S = SIN - K + 1
NT = B * S
H = 256
KH, MH = H // P, H // P
C = 15
NCH = S // C
TT = C * B
CT = 4
CONVN = CT * TT
NCONV = -(-NT // CONVN)
LEVELS = 8
NODES = 2 ** LEVELS - 1
INNER = NODES // 2
LEAVES = 2 ** (LEVELS - 1)
WROWS = CH + 1
WCOLS = LEVELS * CH
WIN = 64
NPAIR = -(-((NT + LEAVES * (WIN - 1)) // WIN) // 2)
NWIN = 2 * NPAIR
NSLOT = NWIN * WIN
RES, XP, PW, IDX = 0, CH, 2 * CH, 2 * CH + LEVELS
ROW = IDX + 1
NOBODY = 16384
WSCALE = 256.0
EPS = 1e-5
PI = 3.141592653589793
TWO_PI_HIGH = 6.28125
TWO_PI_LOW = 2 * PI - TWO_PI_HIGH
ROUND = 1.5 * 2 ** 23
NORM_LINKS = 4
MASK_LINKS = 13
N_POOL_SETUP = 23
WQ = 4
N_TABLE_DMAS = sum(1 + min(2 ** l, LEAVES >> l) for l in range(LEVELS))

assert NCH * C == S


def conv_tokens(i):
    return min(CONVN, NT - i * CONVN)


def stages(c):
    return dict(rec0=c < NCH, rec1=0 <= c - 2 < NCH, fc=0 <= c - 3 < NCH, in1=0 <= c - 1 < NCH,
                in0=c + 1 < NCH, norm=0 <= c - 4 < NCH, path=0 <= c - 5 < NCH)


FIRST_FULL = 7
PAIRS = (NCH - 1 - FIRST_FULL) // 2


def run_chunks(eng, chunk):
    for c in range(FIRST_FULL):
        chunk(c, c % 2, stages(c))
    with eng.Fori(0, PAIRS) as j:
        chunk(FIRST_FULL + 2 * j, 1, stages(FIRST_FULL))
        chunk(FIRST_FULL + 1 + 2 * j, 0, stages(FIRST_FULL))
    for c in range(FIRST_FULL + 2 * PAIRS, NCH + 5):
        chunk(c, c % 2, stages(c))


NB = 8
AHEAD = 5
HEAD = NB + NPAIR % NB
LOOPS = (NPAIR - HEAD) // NB - 1


def run_pairs(eng, pair):
    for w in range(HEAD):
        pair(w, w % NB, w // NB)
    with eng.Fori(0, LOOPS) as j:
        for i in range(HEAD, HEAD + NB):
            pair(NB * j + i, i % NB, j + i // NB)
    for w in range(HEAD + LOOPS * NB, NPAIR):
        pair(w, w % NB, w // NB)


def is_known(number, value):
    return isinstance(number, int) and number == value


def tile_of(t, tensor):
    return tensor[:, bass.ds(t, 1), :].rearrange("p a c -> p (a c)")


def tower(nc, xT, w_real, w_imag, phases, wih0, whh0, bih0, bhh0, wih1, whh1, bih1, bhh1,
          fcw, fcb, w1, b1, w2, b2, out):
    w_leaf = nc.dram_tensor("w_leaf", (LEAVES * WROWS, 2 * WCOLS), F16, kind="Internal").ap()
    sorted_in = nc.dram_tensor("sorted_in", (NSLOT, ROW), F32, kind="Internal").ap()

    with ExitStack() as ctx:
        def sb(name, shape, dt=F32):
            return ctx.enter_context(nc.sbuf_tensor(name, shape, dt))

        def sem(name):
            return ctx.enter_context(nc.semaphore(name))

        x2 = sb("x2", [P, SIN * B])
        wr = sb("wr", [P, K // 2, CH])
        wi = sb("wi", [P, K // 2, CH])
        ph = sb("ph", [P, K // 2])
        trig = sb("trig", [P, 2, K // 2])
        turns = sb("turns", [P, 2, K // 2])
        wc = sb("wc", [P, K // 2, 2, CH])
        wtmp = sb("wtmp", [P, K // 2, CH])
        w_f32 = sb("w_f32", [P, 4, 2 * H])
        fc_f32 = sb("fc_f32", [P, KH, CH])
        bias_f32 = sb("bias_f32", [1, 4, H])
        fcb_f32 = sb("fcb_f32", [1, CH])
        wih0_hi = sb("wih0_hi", [P, H], F16)
        wih0_lo = sb("wih0_lo", [CH + 2, H], F16)
        whh0_p = sb("whh0_p", [P, 2, KH * H], F16)
        wih1_p = sb("wih1_p", [P, 2, KH * H], F16)
        whh1_p = sb("whh1_p", [P, 2, KH * H], F16)
        fc_p = sb("fc_p", [P, 2, KH * CH], F16)
        bias_s = sb("bias_s", [1, 2, H])
        bias_p = sb("bias_p", [1, 2, 2, H], F16)
        bias1_2 = sb("bias1_2", [2, H], F16)
        fcb_p = sb("fcb_p", [1, 2, CH], F16)
        fcb_2 = sb("fcb_2", [2, CH], F16)
        ones_2 = sb("ones_2", [2, P], F16)
        w1_f = sb("w1_f", [P, NODES])
        b1_f = sb("b1_f", [1, NODES])
        b1_p = sb("b1_p", [1, 2, NODES], F16)
        w1_hi = sb("w1_hi", [P, NODES], F16)
        w1_lo = sb("w1_lo", [CH + 2, NODES], F16)
        w2_f = sb("w2_f", [P, 2, LEAVES // WQ * CH])
        w2_p = sb("w2_p", [P, LEAVES, 2, CH], F16)
        b2_f = sb("b2_f", [P, 2, CH])
        b2_p = sb("b2_p", [P, 2, 2, CH], F16)
        ident = sb("ident", [P, P])
        ident_h = sb("ident_h", [P, P], F16)
        mean_w = sb("mean_w", [CH, P])
        before = sb("before", [TT, P], BF16)
        ones_bf = sb("ones_bf", [TT, P], BF16)
        ones_f = sb("ones_f", [P, P])
        win_no = sb("win_no", [P, NWIN])
        eps_t = sb("eps_t", [TT, 1])
        mhalf = sb("mhalf", [TT, 1])
        descale = sb("descale", [TT, LEVELS])
        empty = sb("empty", [P, ROW])
        first_p = sb("first_p", [P, 1])
        conv_work = sb("conv_work", [P, 10, CONVN])
        cv, dev, sq, var, srt = [conv_work[:, 2 * n:2 * n + 2, :] for n in range(5)]
        rcp = sb("rcp", [P, CONVN])
        newton = sb("newton", [P, CONVN])
        x1s = sb("x1s", [P, NT], F16)
        x1b = sb("x1b", [CH + 2, NT], F16)
        h_hi = [sb(f"h{l}_hi", [P, 2, KH, TT], F16) for l in range(2)]
        h_lo = [sb(f"h{l}_lo", [P, 2, KH, TT], F16) for l in range(2)]
        h_f = [sb(f"h{l}_f", [P, KH, B]) for l in range(2)]
        xrow = sb("xrow", [TT, NCH, ROW])
        st = sb("st", [TT, 6])
        mv = sb("mv", [TT, 2])
        rs2 = sb("rs2", [TT, 1])
        d2 = sb("d2", [TT, CH])
        xn = sb("xn", [TT, CH])
        xp = sb("xp", [TT, 2, CH], F16)
        xpT = sb("xpT", [P, TT], F16)
        xbT = sb("xbT", [CH + 2, TT], F16)
        sc = [sb(f"sc{q}", [TT, NODES]) for q in range(2)]
        mask = [sb(f"mask{q}", [TT, NODES]) for q in range(2)]
        right = sb("right", [TT, INNER])
        picked = sb("picked", [TT, NODES])
        plog = sb("plog", [TT, LEVELS])
        pws = sb("pws", [TT, LEVELS])
        mask_bf = conv_work[0:TT, :, :].rearrange("p a n -> p (a n)")[:, 0:NCH * LEAVES // 2].bitcast(BF16).rearrange(
            "p (t f) -> p t f", f=LEAVES)
        rk = sb("rk", [P, 2, LEAVES])
        rkm = sb("rkm", [TT, LEAVES])
        rkr = sb("rkr", [TT, LEAVES])
        rank_t = sb("rank_t", [TT, 1])
        rank = sb("rank", [TT, NCH])
        cnt = sb("cnt", [P, LEAVES])
        cnt_i = sb("cnt_i", [P, LEAVES], I32)
        wins = sb("wins", [P, LEAVES])
        cums = sb("cums", [P, 2, LEAVES])
        base = sb("base", [P, LEAVES])
        cumT = sb("cumT", [P, 1])
        past = rcp[:, 0:NWIN]
        leaf_of = sb("leaf_of", [1, NPAIR, 2])
        pair_leaves = sb("pair_leaves", [1, NPAIR], I32)
        posb = sb("posb", [TT, NCH])
        pos = sb("pos", [TT, NCH], I32)
        used = [0]

        def over_x2(rows, words):
            used[0] += words
            return x2[0:rows, used[0] - words:used[0]]

        posm = conv_work[0:TT, :, :].rearrange("p a n -> p (a n)")[:, NCH * LEAVES // 2:NCH * LEAVES // 2 + 7 * LEAVES] \
            .rearrange("p (t f) -> p t f", f=LEAVES)
        work = [over_x2(P, WCOLS + ROW) for i in range(NB)]
        xs = [wk[:, WCOLS:] for wk in work]
        os_ = [over_x2(P, CH) for i in range(NB)]
        xsT = [w_f32[0:WROWS, i // 4, (i % 4) * P:(i % 4 + 1) * P].bitcast(F16).rearrange("r (a n) -> r a n", a=2)
               for i in range(NB)]
        wl = [[w2_p[0:WROWS, (2 * i + h) * LEVELS:(2 * i + h + 1) * LEVELS, :, :] for h in range(2)]
              for i in range(NB)]
        assert used[0] <= SIN * B
        ix = [sb(f"ix{i}", [P, 1], I32) for i in range(NB)]

        banks = [ctx.enter_context(nc.psum_tensor(f"bank{i}", [P, 512], F32)) for i in range(8)]
        pre = [[banks[0], banks[1]], [banks[2], banks[3]]]
        p_fc, p_tr, p_sc, p_rk = banks[4], banks[5], banks[6], banks[7]
        p_conv, p_mean, p_var, p_h = banks[0:2], banks[2:4], banks[4:6], banks[6:8]
        p_xT = [banks[0][:, :].bitcast(F16), banks[1][:, :].bitcast(F16)]
        p_y = [banks[2], banks[3]]
        p_trh = p_tr[:, :].bitcast(F16)

        s_x, s_xb, s_wc, s_wload, s_w1load, s_b2load, s_pool, s_trig, s_sin, s_wconv = [sem(n) for n in (
            "x_first_half x_second_half wconv_loaded w_loaded w1_loaded b2_loaded pool_setup trig_ready "
            "sin_done wconv_ready").split()]
        s_split, s_rows, s_w2s, s_w2p, s_b2p, s_fill, s_leafw = [sem(n) for n in (
            "split_done part_rows_moved w2_step w2_parts_ready b2_parts_ready slots_emptied leafw_filled").split()]
        s_conv, s_cv, s_mean, s_dev, s_sqd, s_vard, s_vare, s_srt, s_x1, s_x1b, s_tr1, s_hc = [sem(n) for n in (
            "conv_done cv_copied mean_done dev_ready squares_ready var_done var_eps_ready sqrt_ready "
            "x1_ready x1b_ready conv_transposed conv_rows_ready").split()]
        s_mm = [sem(f"rec{l}_done") for l in range(2)]
        s_hi = [sem(f"h{l}_high_ready") for l in range(2)]
        s_lo = [sem(f"h{l}_low_ready") for l in range(2)]
        s_fc, s_h2, s_bn, s_stat, s_xp, s_xrow, s_xpT, s_xpTc, s_sc, s_scc = [sem(n) for n in (
            "fc_done h2_ready bn_ready stats_ready xp_ready xrow_ready xp_transposed xpT_copied scores_done "
            "scores_copied").split()]
        s_mask, s_m7, s_lev, s_plog, s_pw, s_pws, s_rk, s_rkc, s_rkm, s_cnt, s_rankt, s_rank = [sem(n) for n in (
            "masks_ready leaf_mask_ready level_scores plog_ready pw_ready pw_scaled rank_done rank_copied "
            "rkm_ready cnt_ready rank_t_ready rank_ready").split()]
        s_norm_link, s_mask_link, s_dchain = sem("pool_norm_step"), sem("pool_mask_step"), sem("dve_step")
        s_cum, s_cumT, s_past, s_leafp, s_leaves, s_pos, s_scat = [sem(n) for n in (
            "cum_ready cumT_done past_ready winleaf_done leaves_ready pos_ready rows_scattered").split()]
        s_w2load = [sem(f"w2_loaded{i}") for i in range(2)]
        s_xs = [sem(f"xs{i}_loaded") for i in range(NB)]
        s_wl = [sem(f"wl{i}_loaded") for i in range(NB)]
        s_out = [sem(f"os{i}_stored") for i in range(NB)]
        s_xt, s_xtc, s_ixc, s_y, s_prod, s_o = [sem(n) for n in (
            "xsT_done xsT_copied ix_copied y_done prod_done o_ready").split()]
        s_passed = sem("passed")

        block = ctx.enter_context(nc.Block())

        @block.sync
        def _(sp):
            sp.dma_start(ph[0:CH, :], phases[0:1, :].broadcast_to([CH, K // 2])).then_inc(s_wc, 16)
            sp.dma_start(ph[CH:P, :], phases[1:2, :].broadcast_to([CH, K // 2])).then_inc(s_wc, 16)
            sp.dma_start(wr[:, :, :], w_real).then_inc(s_wc, 16)
            sp.dma_start(wi[:, :, :], w_imag).then_inc(s_wc, 16)
            half = (SIN * B) // 2
            sp.dma_start(x2[0:CH, 0:half], xT[:, 0:half]).then_inc(s_x, 16)
            sp.dma_start(x2[CH:P, 0:half], xT[:, B:half + B]).then_inc(s_x, 16)
            sp.dma_start(x2[0:CH, half:], xT[:, half:]).then_inc(s_xb, 16)
            sp.dma_start(x2[CH:P, half:SIN * B - B], xT[:, half + B:]).then_inc(s_xb, 16)
            sp.dma_start(w_f32[0:CH, 0, 0:H], wih0).then_inc(s_wload, 16)
            sp.dma_start(w_f32[CH:P, 0, 0:H], wih0).then_inc(s_wload, 16)
            for n, w in ((1, whh0), (2, wih1), (3, whh1)):
                sp.dma_start(w_f32[:, n, :].rearrange("p (k h) -> p k h", k=KH),
                             w.rearrange("(k p) h -> p k h", p=P)).then_inc(s_wload, 16)
            sp.dma_start(fc_f32[:, :, :], fcw.rearrange("(k p) h -> p k h", p=P)).then_inc(s_wload, 16)
            for n, b in enumerate((bih0, bhh0, bih1, bhh1)):
                sp.dma_start(bias_f32[0:1, n, :], b).then_inc(s_wload, 16)
            sp.dma_start(fcb_f32[0:1, :], fcb).then_inc(s_wload, 16)
            for half in range(2):
                sp.dma_start(w1_f[half * CH:(half + 1) * CH, :], w1).then_inc(s_w1load, 16)
            sp.dma_start(b1_f[0:1, :], b1).then_inc(s_w1load, 16)
            sp.dma_start(b2_f[0:INNER, 0, :], b2[0:INNER, :]).then_inc(s_b2load, 16)
            sp.dma_start(b2_f[:, 1, :], b2[INNER:, :]).then_inc(s_b2load, 16)
            for g in range(WQ):
                n = LEAVES // WQ
                if g >= 2:
                    sp.wait_ge(s_w2p, g - 1)
                up = min(n, INNER - g * n)
                dst = w2_f[:, g % 2, :].rearrange("p (n o) -> p n o", o=CH)
                sp.dma_start(dst[0:CH, 0:up, :],
                             w2[g * n:g * n + up, :, :].rearrange("n d o -> d n o")).then_inc(s_w2load[g % 2], 16)
                sp.dma_start(dst[CH:P, :, :],
                             w2[INNER + g * n:INNER + (g + 1) * n, :, :].rearrange("n d o -> d n o")).then_inc(s_w2load[g % 2], 16)
            sp.wait_ge(s_split, 1)
            for p in range(2):
                sp.dma_start(wih0_lo[CH + p:CH + p + 1, :], bias_p[0:1, p, 0, :]).then_inc(s_rows, 16)
                sp.dma_start(bias1_2[p:p + 1, :], bias_p[0:1, p, 1, :]).then_inc(s_rows, 16)
                sp.dma_start(fcb_2[p:p + 1, :], fcb_p[0:1, p, :]).then_inc(s_rows, 16)
                sp.dma_start(w1_lo[CH + p:CH + p + 1, :], b1_p[0:1, p, :]).then_inc(s_rows, 16)
            sp.wait_ge(s_pool, N_POOL_SETUP)
            sp.dma_start(sorted_in.rearrange("(w p) c -> p w c", p=P),
                         empty[:, :].unsqueeze(1).broadcast_to([P, NPAIR, ROW])).then_inc(s_fill, 16)
            sp.wait_ge(s_w2p, WQ)
            sp.wait_ge(s_b2p, 1)
            table = w_leaf.rearrange("(f r) c -> r f c", r=WROWS)
            for l in range(LEVELS):
                last = l == LEVELS - 1
                n0, n, rep = (0 if last else 2 ** l - 1), 2 ** l, LEAVES >> l
                cols = slice(l * 2 * CH, (l + 1) * 2 * CH)
                rows = slice(CH, P) if last else slice(0, CH)
                level = w2_p[rows, n0:n0 + n, :, :].rearrange("d n a o -> d n (a o)")
                if n < rep:
                    for m in range(n):
                        sp.dma_start(table[0:CH, m * rep:(m + 1) * rep, cols],
                                     level[:, m:m + 1, :].broadcast_to([CH, rep, 2 * CH])).then_inc(s_leafw, 16)
                else:
                    for m in range(rep):
                        sp.dma_start(table[0:CH, m::rep, cols], level).then_inc(s_leafw, 16)
                sp.dma_start(table[CH, :, cols].rearrange("(n r) c -> n r c", r=rep),
                             b2_p[n0:n0 + n, int(last), :, :].rearrange("n a o -> n (a o)").unsqueeze(1)
                             .broadcast_to([n, rep, 2 * CH])).then_inc(s_leafw, 16)

            sp.wait_ge(s_leafw, 16 * N_TABLE_DMAS)
            sp.wait_ge(s_leaves, 1)

            def matrices(w, b, uses):
                leaves = sp.value_load(pair_leaves[0:1, bass.ds(w, 1)])
                if not is_known(uses, 0):
                    sp.wait_ge(s_y, w - NB + 1)
                for h, leaf in enumerate((leaves % LEAVES, leaves // LEAVES)):
                    sp.dma_start(wl[b][h].rearrange("r l a o -> r (l a o)"),
                                 w_leaf[bass.ds(leaf * WROWS, WROWS), :]).then_inc(s_wl[b], 16)

            def load(w, b, uses):
                if not is_known(uses, 0):
                    matrices(w, b, uses)

            for b in range(NB):
                matrices(b, b, 0)
            run_pairs(sp, load)

        @block.gpsimd
        def _(pool):
            done = [0]

            def setup(ins):
                done[0] += 1
                ins.then_inc(s_pool, 1)
                pool.wait_ge(s_pool, done[0])

            setup(pool.memset(mean_w[:, :], 1.0 / CH))
            setup(pool.memset(ident[:, :], 0.0))
            setup(pool.affine_select(out=ident[:, :], in_=ident[:, :], compare_op=ALU.not_equal, fill=1.0,
                                     base=0, pattern=[[-1, P]], channel_multiplier=1))
            setup(pool.tensor_copy(ident_h[:, :], ident[:, :]))
            setup(pool.memset(x1b[CH:CH + 2, :], 1.0))
            setup(pool.memset(xbT[CH:CH + 2, :], 1.0))
            setup(pool.memset(ones_2[:, :], 1.0))
            setup(pool.memset(ones_f[:, :], 1.0))
            setup(pool.memset(ones_bf[:, :], 1.0))
            setup(pool.memset(before[:, :], 0.0))
            setup(pool.affine_select(out=before[:, :], in_=before[:, :], compare_op=ALU.is_ge, fill=1.0,
                                     base=0, pattern=[[-1, P]], channel_multiplier=1))
            setup(pool.memset(first_p[:, :], 0.0))
            setup(pool.affine_select(out=first_p[:, :], in_=first_p[:, :], compare_op=ALU.not_equal, fill=1.0,
                                     base=0, pattern=[[-1, 1]], channel_multiplier=1))
            setup(pool.memset(eps_t[:, :], EPS))
            setup(pool.memset(mhalf[:, :], -0.5))
            setup(pool.memset(descale[:, :], 1 / WSCALE))
            setup(pool.memset(empty[:, :], 0.0))
            setup(pool.memset(empty[:, IDX:IDX + 1].bitcast(I32), NOBODY))
            setup(pool.memset(cnt[:, :], 0.0))
            for q in range(2):
                setup(pool.memset(mask[q][:, 0:1], 1.0))
            setup(pool.iota(win_no[:, :], pattern=[[1, NWIN]], base=0, channel_multiplier=0,
                            allow_small_or_imprecise_dtypes=True))
            setup(pool.iota(xrow[:, :, IDX:IDX + 1].bitcast(I32), pattern=[[TT, NCH], [1, 1]], base=0,
                            channel_multiplier=1))
            assert done[0] == N_POOL_SETUP, done[0]
            step = [0]

            def link(ins):
                step[0] += 1
                ins.then_inc(s_w2s, 1)
                pool.wait_ge(s_w2s, step[0])

            pool.wait_ge(s_b2load, 32)
            for half, rows in ((0, slice(0, INNER)), (1, slice(0, P))):
                link(pool.tensor_scalar(b2_f[rows, half, :], b2_f[rows, half, :], WSCALE, None, ALU.mult))
                link(pool.tensor_copy(b2_p[rows, half, 0, :], b2_f[rows, half, :]))
                last = pool.tensor_tensor(b2_p[rows, half, 1, :], b2_f[rows, half, :], b2_p[rows, half, 0, :],
                                          ALU.subtract)
                if half == 0:
                    link(last)
            last.then_inc(s_b2p, 1)
            pool.wait_ge(s_b2p, 1)
            n = LEAVES // WQ
            for g in range(WQ):
                pool.wait_ge(s_w2load[g % 2], 32 * (g // 2 + 1))
                parts = [(P, n)] if g < WQ - 1 else [(P, n - 1), (None, 1)]
                for m, (rows_n, k) in enumerate(parts):
                    rows = slice(0, P) if rows_n else slice(CH, P)
                    k0 = 0 if rows_n else n - 1
                    src = w2_f[rows, g % 2, k0 * CH:(k0 + k) * CH].rearrange("p (n o) -> p n o", o=CH)
                    dst = w2_p[rows, g * n + k0:g * n + k0 + k, :, :]
                    link(pool.tensor_scalar(src, src, WSCALE, None, ALU.mult))
                    link(pool.tensor_copy(dst[:, :, 0, :], src))
                    last = pool.tensor_tensor(dst[:, :, 1, :], src, dst[:, :, 0, :], ALU.subtract)
                    if m < len(parts) - 1:
                        link(last)
                last.then_inc(s_w2p, 1)
                pool.wait_ge(s_w2p, g + 1)

            def norm(t, q):
                step = [0]

                def link(ins):
                    step[0] += 1
                    ins.then_inc(s_norm_link, 1)
                    pool.wait_ge(s_norm_link, t * NORM_LINKS + step[0])

                pool.wait_ge(s_stat, t + 1)
                link(pool.tensor_tensor(rs2[:, :], mv[:, 1:2], eps_t[:, :], ALU.add))
                link(pool.tensor_tensor(rs2[:, :], rs2[:, :], mhalf[:, :], ALU.pow))
                link(pool.tensor_tensor(d2[:, :], tile_of(t, xrow)[:, RES:XP], mv[:, 0:1].broadcast_to([TT, CH]),
                                        ALU.subtract))
                link(pool.tensor_tensor(xn[:, :], d2[:, :], rs2[:, :].broadcast_to([TT, CH]), ALU.mult))
                pool.sem_inc(s_passed, 1)
                pool.tensor_copy(xp[:, 0, :], xn[:, :]).then_inc(s_xp, 1)
                pool.wait_ge(s_xp, 2 * t + 1)
                pool.tensor_tensor(xp[:, 1, :], xn[:, :], xp[:, 0, :], ALU.subtract).then_inc(s_xp, 1)
                pool.wait_ge(s_xp, 2 * t + 2)
                pool.sem_inc(s_passed, 1)
                pool.tensor_copy(tile_of(t, xrow)[:, XP:PW].bitcast(F16),
                                 xp[:, :, :].rearrange("p a c -> p (a c)")).then_inc(s_xrow, 1)
                assert step[0] == NORM_LINKS

            def masks(t, q):
                step = [0]

                def link(ins):
                    step[0] += 1
                    ins.then_inc(s_mask_link, 1)
                    pool.wait_ge(s_mask_link, t * MASK_LINKS + step[0])

                pool.wait_ge(s_scc, t + 1)
                pool.sem_inc(s_passed, 1)
                link(pool.tensor_scalar(right[:, :], sc[q][:, 0:INNER], 0.0, None, ALU.is_gt))
                for l in range(LEVELS - 1):
                    a, n = 2 ** l - 1, 2 ** l
                    kids = mask[q][:, 2 * n - 1:4 * n - 1].rearrange("p (n t) -> p n t", t=2)
                    yes = pool.tensor_tensor(kids[:, :, 1], mask[q][:, a:a + n], right[:, a:a + n], ALU.mult)
                    link(yes)
                    no = pool.tensor_tensor(kids[:, :, 0], mask[q][:, a:a + n], kids[:, :, 1], ALU.subtract)
                    if l < LEVELS - 3:
                        link(no)
                    else:
                        no.then_inc(s_mask, 1)
                        if l == LEVELS - 3:
                            pool.wait_ge(s_mask, 2 * t + 1)
                pool.wait_ge(s_mask, 2 * t + 2)
                pool.tensor_copy(tile_of(t, mask_bf), mask[q][:, INNER:NODES]).then_inc(s_m7, 1)
                assert step[0] == MASK_LINKS, step[0]

            def ranks(t, q):
                pool.wait_ge(s_rkc, t + 1)
                if not (isinstance(t, int) and t == 0):
                    pool.wait_ge(s_rank, t)
                pool.tensor_tensor(rkm[:, :], rk[0:TT, 0, :], cnt[0:TT, :], ALU.add).then_inc(s_rkm, 1)
                pool.wait_ge(s_rkm, t + 1)
                pool.tensor_tensor(cnt[:, :], cnt[:, :], rk[:, 1, :], ALU.add).then_inc(s_cnt, 1)
                pool.wait_ge(s_cnt, t + 1)

            def chunk(c, q, on):
                if on["norm"]:
                    norm(c - 4, q)
                if on["path"]:
                    ranks(c - 5, 1 - q)
                if on["norm"]:
                    masks(c - 4, q)

            pool.wait_ge(s_hc, NCONV)
            run_chunks(pool, chunk)

            for i in range(NB):
                pool.memset(xsT[i][CH:WROWS, 0, :], 1.0).then_inc(s_pool, 1)
            pool.wait_ge(s_pool, N_POOL_SETUP + NB)
            pool.wait_ge(s_fill, 16)
            pool.wait_ge(s_pws, NCH)
            pool.wait_ge(s_xrow, NCH)
            for t in range(NCH):
                if t % 7 == 0:
                    pool.wait_ge(s_pos, t // 7 + 1)
                pool.indirect_dma_start(sorted_in, bass.IndirectOffsetOnAxis(ap=pos[:, t:t + 1], axis=0),
                                        xrow[:, t, :], None).then_inc(s_scat, 16)

            def store(w, b, uses):
                pool.wait_ge(s_ixc, w + 1)
                pool.wait_ge(s_o, w + 1)
                pool.sem_inc(s_passed, 1)
                pool.indirect_dma_start(out, bass.IndirectOffsetOnAxis(ap=ix[b][:, 0:1], axis=0), os_[b], None,
                                        bounds_check=NT - 1, oob_is_err=False).then_inc(s_out[b], 16)

            run_pairs(pool, store)
            for b in range(NB):
                pool.wait_ge(s_out[b], 16 * len(range(b, NPAIR, NB)))

        @block.vector
        def _(dve):
            v = nc.vector
            chain = [0]

            def link(ins):
                chain[0] += 1
                ins.then_inc(s_dchain, 1)
                dve.wait_ge(s_dchain, chain[0])

            dve.wait_ge(s_wc, 64)
            link(v.tensor_scalar(trig[:, 0, :], ph[:, :], PI / 2, None, ALU.add))
            link(v.tensor_copy(trig[:, 1, :], ph[:, :]))
            link(v.tensor_scalar(turns[:, :, :], trig[:, :, :], 1 / (2 * PI), ROUND, ALU.mult, ALU.add))
            link(v.tensor_scalar(turns[:, :, :], turns[:, :, :], ROUND, None, ALU.subtract))
            link(v.scalar_tensor_tensor(trig[:, :, :], turns[:, :, :], -TWO_PI_HIGH, trig[:, :, :],
                                        ALU.mult, ALU.add))
            link(v.scalar_tensor_tensor(trig[:, :, :], turns[:, :, :], -TWO_PI_LOW, trig[:, :, :],
                                        ALU.mult, ALU.add))
            v.tensor_scalar(trig[:, :, :], trig[:, :, :], 3.1415925, -3.1415925, ALU.min, ALU.max).then_inc(s_trig, 1)
            dve.wait_ge(s_sin, 1)
            for k in range(K // 2):
                link(v.tensor_scalar(wtmp[:, k, :], wi[:, k, :], trig[:, 1, k:k + 1], None, ALU.mult))
                for half in range(2):
                    v.scalar_tensor_tensor(wc[:, k, half, :], wr[:, k, :], trig[:, 0, k:k + 1], wtmp[:, k, :],
                                           ALU.mult, ALU.subtract).then_inc(s_wconv, 1)
            dve.wait_ge(s_wload, 16 * 11)
            dve.wait_ge(s_w1load, 48)
            link(v.tensor_tensor(bias_s[0:1, 0, :], bias_f32[0:1, 0, :], bias_f32[0:1, 1, :], ALU.add))
            link(v.tensor_tensor(bias_s[0:1, 1, :], bias_f32[0:1, 2, :], bias_f32[0:1, 3, :], ALU.add))
            for hi, lo, full in (
                    (wih0_hi[:, :], wih0_lo[0:CH, :], w_f32[:, 0, 0:H]),
                    (w1_hi[:, :], w1_lo[0:CH, :], w1_f[:, :]),
                    (b1_p[0:1, 0, :], b1_p[0:1, 1, :], b1_f[0:1, :]),
                    (whh0_p[:, 0, :], whh0_p[:, 1, :], w_f32[:, 1, :]),
                    (wih1_p[:, 0, :], wih1_p[:, 1, :], w_f32[:, 2, :]),
                    (whh1_p[:, 0, :], whh1_p[:, 1, :], w_f32[:, 3, :]),
                    (fc_p[:, 0, :], fc_p[:, 1, :], fc_f32[:, :, :].rearrange("p k c -> p (k c)")),
                    (fcb_p[:, 0, :], fcb_p[:, 1, :], fcb_f32[0:1, :]),
                    (bias_p[:, 0, :, :].rearrange("p l h -> p (l h)"), bias_p[:, 1, :, :].rearrange("p l h -> p (l h)"),
                     bias_s[:, :, :].rearrange("p l h -> p (l h)"))):
                n = lo.shape[0]
                link(v.tensor_scalar(hi, full, WSCALE, None, ALU.mult))
                link(v.scalar_tensor_tensor(lo, full[0:n], WSCALE, hi[0:n], ALU.mult, ALU.subtract))
            v.memset(turns[:, :, :], 0.0).then_inc(s_split, 1)

            for i in range(NCONV):
                j, n = i % 2, conv_tokens(i)
                tok = slice(i * CONVN, i * CONVN + n)
                dve.wait_ge(s_mean, i + 1)
                if i >= 2:
                    dve.wait_ge(s_x1, i - 1)
                v.tensor_tensor(dev[:, j, 0:n], cv[:, j, 0:n], p_mean[j][:, 0:n], ALU.subtract).then_inc(s_dev, 1)
                dve.wait_ge(s_vard, i + 1)
                v.tensor_scalar(var[:, j, 0:n], p_var[j][:, 0:n], EPS, None, ALU.add).then_inc(s_vare, 1)
                dve.wait_ge(s_srt, i + 1)
                r, y = rcp[:, 0:n], newton[:, 0:n]
                link(v.reciprocal(r, srt[:, j, 0:n]))
                link(v.scalar_tensor_tensor(y, r, -0.5, var[:, j, 0:n], ALU.mult, ALU.mult))
                link(v.tensor_tensor(y, y, r, ALU.mult))
                link(v.scalar_tensor_tensor(r, y, 1.5, r, ALU.add, ALU.mult))
                link(v.tensor_tensor(dev[:, j, 0:n], dev[:, j, 0:n], r, ALU.mult))
                v.tensor_copy(x1b[0:CH, tok], dev[0:CH, j, 0:n]).then_inc(s_x1b, 1)
                link(v.tensor_copy(x1s[:, tok], dev[:, j, 0:n]))
                v.tensor_tensor(x1s[CH:P, tok], dev[CH:P, j, 0:n], x1s[CH:P, tok], ALU.subtract).then_inc(s_x1, 1)

            def low(l, c, k, q):
                dve.wait_ge(s_hi[l], c * C + k + 1)
                col = slice(k * B, (k + 1) * B)
                v.tensor_tensor(h_lo[l][:, q, :, col], h_f[l][:, :, :], h_hi[l][:, q, :, col],
                                ALU.subtract).then_inc(s_lo[l], 1)

            def norm(k, t, q):
                if k == 0:
                    dve.wait_ge(s_fc, t + 1)
                    row = tile_of(t, xrow)[:, RES:XP]
                    v.scalar_tensor_tensor(row, p_fc[0:TT, 0:CH], 1 / WSCALE, row, ALU.mult, ALU.add).then_inc(s_h2, 1)
                elif k == 1:
                    dve.wait_ge(s_h2, t + 1)
                    dve.sem_inc(s_passed, 1)
                    v.bn_stats(st[:, :], tile_of(t, xrow)[:, RES:XP]).then_inc(s_bn, 1)
                elif k == 2:
                    dve.wait_ge(s_bn, t + 1)
                    if not (isinstance(t, int) and t == 0):
                        dve.wait_ge(s_xp, 2 * t)
                    dve.sem_inc(s_passed, 1)
                    v.bn_aggr(mv[:, :], st[:, :]).then_inc(s_stat, 1)

            def path(k, t, q):
                l = k - 4
                if 0 <= l < LEVELS:
                    if l == 0:
                        dve.wait_ge(s_mask, 2 * t + 2)
                        if not (isinstance(t, int) and t == 0):
                            dve.wait_ge(s_pw, t)
                    nodes = slice(2 ** l - 1, 2 ** (l + 1) - 1)
                    v.tensor_tensor_reduce(out=picked[:, nodes], in0=mask[q][:, nodes], in1=sc[q][:, nodes],
                                           scale=1.0, scalar=0.0, op0=ALU.mult, op1=ALU.add,
                                           accum_out=plog[:, l:l + 1]).then_inc(s_lev, 1)
                elif k == 12:
                    dve.wait_ge(s_lev, t * LEVELS + LEVELS)
                    v.scalar_tensor_tensor(plog[:, :], plog[:, :], -1.0, plog[:, :], ALU.mult, ALU.max).then_inc(s_plog, 1)
                elif k == 13:
                    dve.wait_ge(s_rkm, t + 1)
                    v.tensor_tensor_reduce(out=rkr[:, :], in0=rkm[:, :], in1=mask[q][:, INNER:NODES], scale=1.0,
                                           scalar=0.0, op0=ALU.mult, op1=ALU.add,
                                           accum_out=rank_t[:, :]).then_inc(s_rankt, 1)
                elif k == 14:
                    dve.wait_ge(s_rankt, t + 1)
                    v.tensor_tensor(rank[:, bass.ds(t, 1)], rank_t[:, :], rank_t[:, :], ALU.max).then_inc(s_rank, 1)
                    dve.wait_ge(s_pw, t + 1)
                    v.tensor_tensor(tile_of(t, xrow)[:, PW:IDX], pws[:, :], descale[:, :], ALU.mult).then_inc(s_pws, 1)

            def chunk(c, q, on):
                for k in range(C):
                    if on["rec0"]:
                        low(0, c, k, q)
                    if on["norm"]:
                        norm(k, c - 4, q)
                    if on["rec1"]:
                        low(1, c - 2, k, q)
                    if on["path"]:
                        path(k, c - 5, 1 - q)

            run_chunks(dve, chunk)

            dve.wait_ge(s_cnt, NCH)
            link(v.tensor_scalar(wins[:, :], cnt[:, :], float(WIN - 1), None, ALU.add))
            link(v.tensor_copy(cnt_i[:, :], wins[:, :]))
            link(v.tensor_scalar(cnt_i[:, :], cnt_i[:, :], WIN.bit_length() - 1, None, ALU.arith_shift_right))
            link(v.tensor_copy(wins[:, :], cnt_i[:, :]))
            link(v.tensor_copy(cums[:, 0, :], wins[:, :]))
            a, d = 0, 1
            while d < LEAVES:
                v.tensor_copy(cums[:, 1 - a, 0:d], cums[:, a, 0:d])
                link(v.tensor_tensor(cums[:, 1 - a, d:], cums[:, a, d:], cums[:, a, 0:LEAVES - d], ALU.add))
                a, d = 1 - a, 2 * d
            v.tensor_tensor(base[:, :], cums[:, a, :], wins[:, :], ALU.subtract).then_inc(s_cum, 1)
            dve.wait_ge(s_cum, 1)
            link(v.tensor_scalar(base[:, :], base[:, :], float(WIN), None, ALU.mult))
            def slots(g):
                tiles = slice(7 * g, 7 * g + 7)
                link(v.tensor_tensor(posm[:, :, :], mask_bf[:, tiles, :],
                                     base[0:TT, :].unsqueeze(1).broadcast_to([TT, 7, LEAVES]), ALU.mult))
                link(v.tensor_reduce(posb[:, tiles], posm[:, :, :], AX.X, ALU.add))
                v.tensor_tensor(pos[:, tiles], posb[:, tiles], rank[:, tiles], ALU.add).then_inc(s_pos, 1)

            slots(0)
            dve.wait_ge(s_cumT, 1)
            link(v.tensor_copy(cumT[:, :], p_tr[:, 0:1]))
            v.tensor_scalar(past[:, :], win_no[:, :], cumT[:, 0:1], None, ALU.is_ge).then_inc(s_past, 1)
            dve.wait_ge(s_leafp, 1)
            link(v.tensor_scalar(leaf_of[0:1, :, :].rearrange("p w h -> p (w h)"), p_sc[0:1, 0:NWIN],
                                 float(LEAVES - 1), None, ALU.min))
            v.scalar_tensor_tensor(pair_leaves[0:1, :], leaf_of[0:1, :, 1], float(LEAVES), leaf_of[0:1, :, 0],
                                   ALU.mult, ALU.add).then_inc(s_leaves, 1)
            for g in range(1, NCH // 7):
                slots(g)

            def weigh(w, b, uses):
                dve.wait_ge(s_y, w + 1)
                dve.wait_ge(s_xs[b], uses * 16 + 16)
                v.tensor_tensor(work[b][:, 0:WCOLS].rearrange("p (l o) -> p l o", l=LEVELS),
                                p_y[b % 2][:, :].rearrange("p (l o) -> p l o", l=LEVELS),
                                xs[b][:, PW:IDX].unsqueeze(2).broadcast_to([P, LEVELS, CH]),
                                ALU.mult).then_inc(s_prod, 1)

            def pair(w, b, uses):
                if not is_known(w, NPAIR - 1):
                    weigh(w + 1, (b + 1) % NB, uses + (b + 1) // NB)
                dve.wait_ge(s_prod, w + 1)
                if not is_known(uses, 0):
                    dve.wait_ge(s_out[b], uses * 16)
                v.tensor_reduce(os_[b], work[b][:, 0:WCOLS + CH].rearrange("p (l o) -> p o l", l=LEVELS + 1),
                                AX.X, ALU.add).then_inc(s_o, 1)

            weigh(0, 0, 0)
            run_pairs(dve, pair)

        @block.scalar
        def _(act):
            a = nc.scalar
            act.wait_ge(s_trig, 1)
            a.activation(trig[:, :, :], trig[:, :, :], ACT.Sin).then_inc(s_sin, 1)
            a.preload_act_table_set("sqrt_and_others")

            def copy_conv(i):
                j, n = i % 2, conv_tokens(i)
                act.wait_ge(s_conv, i + 1)
                if i >= 2:
                    act.wait_ge(s_dev, i - 1)
                    act.wait_ge(s_tr1, i - 1)
                a.activation(cv[:, j, 0:n], p_conv[j][:, 0:n], ACT.Copy).then_inc(s_cv, 1)

            copy_conv(0)
            for i in range(NCONV):
                j, n, g = i % 2, conv_tokens(i), conv_tokens(i) // TT
                if i + 1 < NCONV:
                    copy_conv(i + 1)
                act.wait_ge(s_dev, i + 1)
                if i >= 2:
                    act.wait_ge(s_vard, i - 1)
                a.activation(sq[:, j, 0:n], dev[:, j, 0:n], ACT.Square).then_inc(s_sqd, 1)
                act.wait_ge(s_tr1, i + 1)
                a.activation(xrow[:, i * CT:i * CT + g, RES:XP], p_h[j][0:TT, 0:g * CH].rearrange(
                    "p (g c) -> p g c", c=CH), ACT.Copy).then_inc(s_hc, 1)
                act.wait_ge(s_vare, i + 1)
                a.activation(srt[:, j, 0:n], var[:, j, 0:n], ACT.Sqrt).then_inc(s_srt, 1)
            a.preload_act_table_set("gelu_and_others")

            def tanh(l, c, k, q):
                act.wait_ge(s_mm[l], c * C + k + 1)
                col = slice(k * B, (k + 1) * B)
                z = pre[l][q][:, 0:MH * TT].rearrange("p (m n) -> p m n", m=MH)[:, :, col]
                a.activation(h_f[l][:, :, :], z, ACT.Tanh, scale=1 / WSCALE)
                a.activation(h_hi[l][:, q, :, col], z, ACT.Tanh, scale=1 / WSCALE).then_inc(s_hi[l], 1)

            def norm(k, t, q):
                if k == 8:
                    act.wait_ge(s_xpT, t + 1)
                    a.activation(xbT[0:CH, :], p_trh[0:CH, 0:TT], ACT.Copy)
                    a.activation(xpT[:, :], p_trh[:, 0:TT], ACT.Copy).then_inc(s_xpTc, 1)
                elif k == 12:
                    act.wait_ge(s_sc, t + 1)
                    a.activation(sc[q][:, :], p_sc[0:TT, 0:NODES], ACT.Copy).then_inc(s_scc, 1)

            def path(k, t, q):
                if k == 6:
                    act.wait_ge(s_rk, t + 1)
                    a.activation(rk[:, :, :].rearrange("p a c -> p (a c)"), p_rk[:, 0:2 * LEAVES],
                                 ACT.Copy).then_inc(s_rkc, 1)
                elif k == 13:
                    act.wait_ge(s_plog, t + 1)
                    if not (isinstance(t, int) and t == 0):
                        act.wait_ge(s_pws, t)
                    a.activation(pws[:, :], plog[:, :], ACT.Gelu, scale=1 / WSCALE).then_inc(s_pw, 1)

            def chunk(c, q, on):
                for k in range(C):
                    if on["rec0"]:
                        tanh(0, c, k, q)
                    if on["path"]:
                        path(k, c - 5, 1 - q)
                    if on["rec1"]:
                        tanh(1, c - 2, k, q)
                    if on["norm"]:
                        norm(k, c - 4, q)

            run_chunks(act, chunk)

            def rows(w, b):
                act.dma_start(xs[b], sorted_in[bass.ds(w * P, P), :]).then_inc(s_xs[b], 16)

            def pair(w, b, uses):
                act.wait_ge(s_xt, w + 1)
                if not is_known(uses, 0):
                    act.wait_ge(s_y, w - NB + 1)
                a.activation(xsT[b][0:CH, :, :].rearrange("p a n -> p (a n)"), p_xT[b % 2][0:CH, 0:2 * P],
                             ACT.Copy).then_inc(s_xtc, 1)
                if not is_known(uses, 0):
                    act.wait_ge(s_out[b], uses * 16)
                a.activation(ix[b][:, :], xs[b][:, IDX:IDX + 1].bitcast(I32), ACT.Copy).then_inc(s_ixc, 1)
                if isinstance(w, int) and w + AHEAD >= NPAIR:
                    return
                if not (isinstance(w, int) and w + AHEAD < NB):
                    act.wait_ge(s_o, w + AHEAD - NB + 1)
                    act.wait_ge(s_ixc, w + AHEAD - NB + 1)
                rows(w + AHEAD, (b + AHEAD) % NB)

            act.wait_ge(s_scat, 16 * NCH)
            for b in range(AHEAD):
                rows(b, b)
            run_pairs(act, pair)

        @block.tensor
        def _(pe):
            mm = nc.tensor.matmul
            pe.wait_ge(s_wconv, K)
            pe.wait_ge(s_pool, N_POOL_SETUP)

            def conv(i):
                n = conv_tokens(i)
                pe.wait_ge(s_x, 32)
                if i * CONVN + n + (K - 1) * B > SIN * B // 2:
                    pe.wait_ge(s_xb, 32)
                if i >= 2:
                    pe.wait_ge(s_cv, i - 1)
                for k in range(K // 2):
                    at = i * CONVN + 2 * k * B
                    last = mm(p_conv[i % 2][:, 0:n], wc[:, k, :, :].rearrange("p a c -> p (a c)"),
                              x2[:, at:at + n], start=(k == 0), stop=(k == K // 2 - 1))
                last.then_inc(s_conv, 1)

            def stats(i):
                j, n = i % 2, conv_tokens(i)
                pe.wait_ge(s_cv, i + 1)
                if i >= 2:
                    pe.wait_ge(s_dev, i - 1)
                mm(p_mean[j][:, 0:n], mean_w[:, :], cv[0:CH, j, 0:n], start=True, stop=True).then_inc(s_mean, 1)
                if i >= 2:
                    pe.wait_ge(s_hc, i - 1)
                for g in range(n // TT):
                    last = nc.tensor.transpose(p_h[j][0:TT, g * CH:(g + 1) * CH], cv[0:CH, j, g * TT:(g + 1) * TT],
                                               ident[0:CH, 0:CH])
                last.then_inc(s_tr1, 1)
                pe.wait_ge(s_sqd, i + 1)
                if i >= 2:
                    pe.wait_ge(s_vare, i - 1)
                mm(p_var[j][:, 0:n], mean_w[:, :], sq[0:CH, j, 0:n], start=True, stop=True).then_inc(s_vard, 1)

            conv(0)
            for i in range(NCONV):
                if i + 1 < NCONV:
                    conv(i + 1)
                stats(i)

            def shared(z, w, x, start=False):
                return mm(z, w, x, start=start, stop=True, skip_group_check=True)

            def in0(n, q, piece):
                m, j = divmod(piece, 2)
                z, ms = pre[0][q][:, m * TT:(m + 1) * TT], slice(m * P, (m + 1) * P)
                cols = bass.ds(n * TT, TT)
                if j == 0:
                    shared(z, wih0_hi[:, ms], x1s[:, cols], start=(piece == 0))
                else:
                    last = shared(z, wih0_lo[:, ms], x1b[:, cols])
                    if m == MH - 1 and isinstance(n, int) and n == 0:
                        last.then_inc(s_mm[0], 1)

            def in1(n, q, piece):
                m, j = divmod(piece, 7)
                z, ms = pre[1][q][:, m * TT:(m + 1) * TT], slice(m * P, (m + 1) * P)
                if j < 6:
                    k, (p, h) = j // 3, ((0, h_hi), (0, h_lo), (1, h_hi))[j % 3]
                    shared(z, wih1_p[:, p, k * H + m * P:k * H + (m + 1) * P], h[0][:, q, k, :],
                           start=(piece == 0))
                else:
                    last = shared(z, bias1_2[:, ms], ones_2[:, 0:TT])
                    if m == MH - 1 and isinstance(n, int) and n == 0:
                        last.then_inc(s_mm[1], 1)

            def fc(t, q, piece):
                z = p_fc[0:TT, 0:CH]
                if piece == 0 and not (isinstance(t, int) and t == 0):
                    pe.wait_ge(s_h2, t)
                if piece < 6:
                    k, (p, h) = piece // 3, ((0, h_hi), (0, h_lo), (1, h_hi))[piece % 3]
                    mm(z, h[1][:, q, k, :], fc_p[:, p, k * CH:(k + 1) * CH], start=(piece == 0), stop=False)
                else:
                    mm(z, ones_2[:, 0:TT], fcb_2[:, :], start=False, stop=True).then_inc(s_fc, 1)

            def turn(t):
                pe.wait_ge(s_xp, 2 * t + 2)
                nc.tensor.transpose(p_trh[:, 0:TT], xp[:, :, :].rearrange("p a c -> p (a c)"),
                                    ident_h[0:TT, 0:TT]).then_inc(s_xpT, 1)

            def scores(t, piece):
                z = p_sc[0:TT, 0:NODES]
                if piece == 0:
                    pe.wait_ge(s_xpTc, t + 1)
                    mm(z, xpT[:, :], w1_hi[:, :], start=True, stop=False)
                else:
                    mm(z, xbT[:, :], w1_lo[:, :], start=False, stop=True).then_inc(s_sc, 1)

            def ranks(t):
                pe.wait_ge(s_m7, t + 1)
                m7 = tile_of(t, mask_bf)
                mm(p_rk[:, 0:LEAVES], before[:, :], m7, start=True, stop=False)
                mm(p_rk[:, LEAVES:2 * LEAVES], ones_bf[:, :], m7, start=False, stop=True).then_inc(s_rk, 1)

            def side(n, c, q, on):
                if n < 4:
                    if on["in0"]:
                        in0(c + 1, 1 - q, n)
                elif n < 9:
                    if on["in1"]:
                        in1(c - 1, 1 - q, n - 4)
                elif n == 9:
                    if on["path"]:
                        ranks(c - 5)
                elif n < 12:
                    if on["in1"]:
                        in1(c - 1, 1 - q, n - 5)
                elif n < 14:
                    if on["fc"]:
                        fc(c - 3, 1 - q, n - 12)
                elif n == 14:
                    if on["norm"]:
                        turn(c - 4)
                elif n < 22:
                    if on["in1"]:
                        in1(c - 1, 1 - q, n - 8)
                elif n < 24:
                    if on["norm"]:
                        scores(c - 4, n - 22)
                elif on["fc"]:
                    fc(c - 3, 1 - q, n - 22)

            def recur(l, c, k, q):
                if k == 0 and isinstance(c, int) and c == 0:
                    return
                w = (whh0_p, whh1_p)[l]
                pq, pk = (q, k - 1) if k else (1 - q, C - 1)
                cols = slice(pk * B, (pk + 1) * B)
                z = [pre[l][q][:, m * TT + k * B:m * TT + (k + 1) * B] for m in range(MH)]
                pe.wait_ge(s_hi[l], c * C + k)
                for p in range(2):
                    for m in range(MH):
                        for kk in range(KH):
                            shared(z[m], w[:, p, kk * H + m * P:kk * H + (m + 1) * P], h_hi[l][:, pq, kk, cols])
                pe.wait_ge(s_lo[l], c * C + k)
                for m in range(MH):
                    for kk in range(KH):
                        last = shared(z[m], w[:, 0, kk * H + m * P:kk * H + (m + 1) * P],
                                      h_lo[l][:, pq, kk, cols])
                last.then_inc(s_mm[l], 1)

            def chunk(c, q, on):
                if on["in1"] and not on["rec0"]:
                    pe.wait_ge(s_hi[0], S)
                    pe.wait_ge(s_lo[0], S)
                if on["fc"] and not on["rec1"]:
                    pe.wait_ge(s_hi[1], S)
                    pe.wait_ge(s_lo[1], S)
                for k in range(C):
                    if on["rec0"]:
                        recur(0, c, k, q)
                    if k:
                        side(2 * k - 1, c, q, on)
                    if on["rec1"]:
                        recur(1, c - 2, k, q)
                    side(2 * k, c, q, on)

            pe.wait_ge(s_split, 1)
            pe.wait_ge(s_rows, 16 * 8)
            pe.wait_ge(s_x1, NCONV)
            pe.wait_ge(s_x1b, NCONV)
            pe.wait_ge(s_hc, NCONV)
            for piece in range(4):
                in0(0, 0, piece)
            run_chunks(pe, chunk)

            pe.wait_ge(s_cum, 1)
            mm(p_tr[:, 0:1], cums[:, 1, :], first_p[:, :], start=True, stop=True).then_inc(s_cumT, 1)
            pe.wait_ge(s_past, 1)
            pe.wait_ge(s_pool, N_POOL_SETUP + NB)
            mm(p_sc[:, 0:NWIN], ones_f[:, :], past[:, :], start=True, stop=True).then_inc(s_leafp, 1)

            def flip(w, b, uses):
                pe.wait_ge(s_xs[b], uses * 16 + 16)
                if not (isinstance(w, int) and w < 2):
                    pe.wait_ge(s_xtc, w - 1)
                pe.sem_inc(s_passed, 1)
                parts = xs[b][:, XP:PW].bitcast(F16)
                nc.tensor.transpose(p_xT[b % 2][0:CH, 0:P], parts[:, 0:CH], ident_h[:, :])
                nc.tensor.transpose(p_xT[b % 2][0:CH, P:2 * P], parts[:, CH:2 * CH], ident_h[:, :]).then_inc(s_xt, 1)

            def pair(w, b, uses):
                if not is_known(w, NPAIR - 1):
                    flip(w + 1, (b + 1) % NB, uses + (b + 1) // NB)
                pe.wait_ge(s_xtc, w + 1)
                pe.wait_ge(s_wl[b], uses * 32 + 32)
                if not (isinstance(w, int) and w < 2):
                    pe.wait_ge(s_prod, w - 1)
                for h in range(2):
                    z = p_y[b % 2][h * WIN:(h + 1) * WIN, :].rearrange("p (l o) -> p l o", l=LEVELS)
                    x = xsT[b][:, :, h * WIN:(h + 1) * WIN]
                    mm(z, x[:, 0, :], wl[b][h][:, :, 0, :], start=True, stop=False)
                    mm(z, x[:, 0, :], wl[b][h][:, :, 1, :], start=False, stop=False)
                    last = mm(z, x[0:CH, 1, :], wl[b][h][0:CH, :, 0, :], start=False, stop=True)
                last.then_inc(s_y, 1)

            flip(0, 0, 0)
            run_pairs(pe, pair)


def kernel(x, L0_tok_w_real, L0_tok_w_imag, L0_tok_phases, L0_attn_W_ih_0, L0_attn_W_hh_0,
           L0_attn_b_ih_0, L0_attn_b_hh_0, L0_attn_W_ih_1, L0_attn_W_hh_1, L0_attn_b_ih_1,
           L0_attn_b_hh_1, L0_attn_fc_w, L0_attn_fc_b, L0_ffn_w1s, L0_ffn_b1s, L0_ffn_w2s, L0_ffn_b2s):
    import numpy as np
    import concourse.bacc as bacc
    from concourse.bass_utils import run_bass_kernel_spmd

    def taps(w):
        return np.asarray(w).transpose(2, 1, 0).reshape(K // 2, 2, CH, CH).transpose(1, 2, 0, 3).reshape(P, K // 2, CH)

    laid_out = {
        "xT": np.asarray(x).transpose(2, 1, 0).reshape(CH, SIN * B),
        "w_real": taps(L0_tok_w_real),
        "w_imag": taps(L0_tok_w_imag),
        "phases": np.asarray(L0_tok_phases).reshape(K // 2, 2).T,
        "wih0": np.asarray(L0_attn_W_ih_0).T,
        "whh0": np.asarray(L0_attn_W_hh_0).T,
        "bih0": np.asarray(L0_attn_b_ih_0).reshape(1, H),
        "bhh0": np.asarray(L0_attn_b_hh_0).reshape(1, H),
        "wih1": np.asarray(L0_attn_W_ih_1).T,
        "whh1": np.asarray(L0_attn_W_hh_1).T,
        "bih1": np.asarray(L0_attn_b_ih_1).reshape(1, H),
        "bhh1": np.asarray(L0_attn_b_hh_1).reshape(1, H),
        "fcw": np.asarray(L0_attn_fc_w).T,
        "fcb": np.asarray(L0_attn_fc_b).reshape(1, CH),
        "w1": np.asarray(L0_ffn_w1s).T,
        "b1": np.asarray(L0_ffn_b1s).reshape(1, NODES),
        "w2": np.asarray(L0_ffn_w2s),
        "b2": np.asarray(L0_ffn_b2s),
    }
    nc = bacc.Bacc("TRN2", target_bir_lowering=False, num_devices=1)
    arrays, args = {}, []
    for name, a in laid_out.items():
        a = np.ascontiguousarray(a)
        arrays[name + "_dram"] = a
        args.append(nc.dram_tensor(name + "_dram", a.shape, mybir.dt.from_np(a.dtype), kind="ExternalInput").ap())
    args.append(nc.dram_tensor("out_dram", (NT, CH), F32, kind="ExternalOutput").ap())
    tower(nc, *args)
    r = run_bass_kernel_spmd(nc, [arrays], core_ids=[0])
    got = r.results[0]["out_dram"]
    return got.reshape(S, B, CH).transpose(1, 0, 2)
```

```python
import concourse.bass as bass
from concourse import mybir
from contextlib import ExitStack

F32 = mybir.dt.float32
F16 = mybir.dt.float16
BF16 = mybir.dt.bfloat16
I32 = mybir.dt.int32
ALU = mybir.AluOpType
ACT = mybir.ActivationFunctionType
AX = mybir.AxisListType

P = 128
B, SIN, CH, K = 8, 750, 64, 16
S = SIN - K + 1
NT = B * S
H = 256
KH, MH = H // P, H // P
C = 15
NCH = S // C
TT = C * B
XCOLS = (SIN - 1) * B
XQ = 4
GT = 7
GROUPS = NCH // GT
LEVELS = 8
NODES = 2 ** LEVELS - 1
INNER = NODES // 2
LEAVES = 2 ** (LEVELS - 1)
WROWS = CH + 1
WCOLS = LEVELS * CH
WIN = 64
NPAIR = -(-((NT + LEAVES * (WIN - 1)) // WIN) // 2)
NWIN = 2 * NPAIR
NSLOT = NWIN * WIN
RES, XP, PW, IDX = 0, CH, 2 * CH, 2 * CH + LEVELS
ROW = IDX + 1
NOBODY = 16384
WSCALE = 256.0
EPS = 1e-5
PI = 3.141592653589793
TWO_PI_HIGH = 6.28125
TWO_PI_LOW = 2 * PI - TWO_PI_HIGH
ROUND = 1.5 * 2 ** 23
NORM_LINKS = 4
MASK_LINKS = 13
N_POOL_SETUP = 26
WQ = 8
N_TABLE_DMAS = sum(1 + min(2 ** l, LEAVES >> l) for l in range(LEVELS))

assert NCH * C == S and GROUPS * GT == NCH and XCOLS % XQ == 0


def stages(c):
    return dict(rec0=c < NCH, rec1=0 <= c - 2 < NCH, fc=0 <= c - 3 < NCH, in1=0 <= c - 1 < NCH,
                in0=c + 1 < NCH, norm=0 <= c - 4 < NCH, path=0 <= c - 5 < NCH)


FIRST_FULL = 7
UNROLL = 4
ROUNDS = (NCH - 1 - FIRST_FULL) // UNROLL


def run_chunks(eng, chunk):
    for c in range(FIRST_FULL):
        chunk(c, c % 2, stages(c))
    with eng.Fori(0, ROUNDS) as j:
        for i in range(FIRST_FULL, FIRST_FULL + UNROLL):
            chunk(UNROLL * j + i, i % 2, stages(FIRST_FULL))
    for c in range(FIRST_FULL + UNROLL * ROUNDS, NCH + 5):
        chunk(c, c % 2, stages(c))


NB = 8
AHEAD = 5
HEAD = NB + NPAIR % NB
LOOPS = (NPAIR - HEAD) // NB - 1


def run_pairs(eng, pair):
    for w in range(HEAD):
        pair(w, w % NB, w // NB)
    with eng.Fori(0, LOOPS) as j:
        for i in range(HEAD, HEAD + NB):
            pair(NB * j + i, i % NB, j + i // NB)
    for w in range(HEAD + LOOPS * NB, NPAIR):
        pair(w, w % NB, w // NB)


def is_known(number, value):
    return isinstance(number, int) and number == value


def tile_of(t, tensor):
    return tensor[:, bass.ds(t, 1), :].rearrange("p a c -> p (a c)")


def tower(nc, xT, w_real, w_imag, phases, wih0, whh0, bih0, bhh0, wih1, whh1, bih1, bhh1,
          fcw, fcb, w1, b1, w2, b2, out):
    w_leaf = nc.dram_tensor("w_leaf", (LEAVES * WROWS, 2 * WCOLS), F16, kind="Internal").ap()
    sorted_in = nc.dram_tensor("sorted_in", (NSLOT, ROW), F32, kind="Internal").ap()

    with ExitStack() as ctx:
        def sb(name, shape, dt=F32):
            return ctx.enter_context(nc.sbuf_tensor(name, shape, dt))

        def sem(name):
            return ctx.enter_context(nc.semaphore(name))

        x2 = sb("x2", [P, XCOLS])
        wr = sb("wr", [P, K // 2, CH])
        wi = sb("wi", [P, K // 2, CH])
        ph = sb("ph", [P, K // 2])
        trig = sb("trig", [P, 2, K // 2])
        turns = sb("turns", [P, 2, K // 2])
        wc = sb("wc", [P, K // 2, CH])
        wc_p = sb("wc_p", [P, K // 2, 2, CH], F16)
        wtmp = sb("wtmp", [P, K // 2, CH])
        w_f32 = sb("w_f32", [P, 4, 2 * H])
        fc_f32 = sb("fc_f32", [P, KH, CH])
        bias_f32 = sb("bias_f32", [1, 4, H])
        fcb_f32 = sb("fcb_f32", [1, CH])
        wih0_hi = sb("wih0_hi", [P, H], F16)
        wih0_lo = sb("wih0_lo", [CH + 2, H], F16)
        whh0_p = sb("whh0_p", [P, 2, KH * H], F16)
        wih1_p = sb("wih1_p", [P, 2, KH * H], F16)
        whh1_p = sb("whh1_p", [P, 2, KH * H], F16)
        fc_p = sb("fc_p", [P, 2, KH * CH], F16)
        bias_s = sb("bias_s", [1, 2, H])
        bias_p = sb("bias_p", [1, 2, 2, H], F16)
        bias1_2 = sb("bias1_2", [2, H], F16)
        fcb_p = sb("fcb_p", [1, 2, CH], F16)
        fcb_2 = sb("fcb_2", [2, CH], F16)
        ones_2 = sb("ones_2", [2, P], F16)
        w1_f = sb("w1_f", [P, NODES])
        b1_f = sb("b1_f", [1, NODES])
        b1_p = sb("b1_p", [1, 2, NODES], F16)
        w1_hi = sb("w1_hi", [P, NODES], F16)
        w1_lo = sb("w1_lo", [CH + 2, NODES], F16)
        w2_f = sb("w2_f", [P, 2, LEAVES // WQ * CH])
        w2_p = sb("w2_p", [P, LEAVES, 2, CH], F16)
        b2_f = sb("b2_f", [P, 2, CH])
        b2_p = sb("b2_p", [P, 2, 2, CH], F16)
        ident_h = sb("ident_h", [P, P], F16)
        before = sb("before", [TT, P], BF16)
        ones_bf = sb("ones_bf", [TT, P], BF16)
        ones_f = sb("ones_f", [P, P])
        win_no = sb("win_no", [P, NWIN])
        eps_t = sb("eps_t", [TT, 1])
        mhalf = sb("mhalf", [TT, 1])
        descale = sb("descale", [TT, LEVELS])
        empty = sb("empty", [P, ROW])
        first_p = sb("first_p", [P, 1])
        x_p = sb("x_p", [P, 2, XCOLS + P - TT], F16)
        stg = sb("stg", [TT, GT, 6])
        mvg = sb("mvg", [TT, GT, 2])
        var = sb("var", [TT, GT])
        srt = sb("srt", [TT, GT])
        rcp = sb("rcp", [TT, GT])
        newton = sb("newton", [TT, GT])
        xng = sb("xng", [TT, GT, CH])
        xpg = sb("xpg", [TT, 2, GT, 2, CH], F16)
        x1s = sb("x1s", [P, NT], F16)
        x1b = sb("x1b", [CH + 2, NT], F16)
        h_hi = [sb(f"h{l}_hi", [P, 2, KH, P], F16) for l in range(2)]
        h_lo = [sb(f"h{l}_lo", [P, 2, KH, P], F16) for l in range(2)]
        h_f = [sb(f"h{l}_f", [P, KH, B]) for l in range(2)]
        xrow = sb("xrow", [TT, NCH, ROW])
        st = sb("st", [TT, 6])
        mv = sb("mv", [TT, 2])
        rs2 = sb("rs2", [TT, 1])
        d2 = sb("d2", [TT, CH])
        xn = sb("xn", [TT, CH])
        xp = sb("xp", [TT, 2, CH], F16)
        xpT = sb("xpT", [P, P], F16)
        xbT = sb("xbT", [CH + 2, P], F16)
        sc = [sb(f"sc{q}", [TT, NODES]) for q in range(2)]
        mask = [sb(f"mask{q}", [TT, NODES]) for q in range(2)]
        right = sb("right", [TT, INNER])
        picked = sb("picked", [TT, NODES])
        plog = sb("plog", [TT, LEVELS])
        pws = sb("pws", [TT, LEVELS])
        over_xp = x_p[0:TT, :, :].rearrange("p a n -> p (a n)")
        mask_bf = over_xp[:, 0:NCH * LEAVES].bitcast(BF16).rearrange("p (t f) -> p t f", f=LEAVES)
        rk = sb("rk", [P, 2, LEAVES])
        rkm = sb("rkm", [TT, LEAVES])
        rkr = sb("rkr", [TT, LEAVES])
        rank_t = sb("rank_t", [TT, 1])
        rank = sb("rank", [TT, NCH])
        cnt = sb("cnt", [P, LEAVES])
        wins = sb("wins", [P, LEAVES])
        cums = w_f32[:, 2, 0:2 * LEAVES].rearrange("p (a f) -> p a f", a=2)
        cnt_i = w_f32[:, 2, 2 * LEAVES:3 * LEAVES].bitcast(I32)
        base = w_f32[:, 2, 3 * LEAVES:4 * LEAVES]
        cumT = sb("cumT", [P, 1])
        past = w_f32[:, 3, 0:NWIN]
        leaf_of = w_f32[0:1, 3, NWIN:2 * NWIN].rearrange("p (w h) -> p w h", h=2)
        pair_leaves = sb("pair_leaves", [1, NPAIR], I32)
        four_leaves = w_f32[0:1, 1, 0:NPAIR // 2].bitcast(I32)
        posb = w_f32[0:TT, 3, 2 * NWIN:2 * NWIN + NCH]
        pos = sb("pos", [TT, NCH], I32)
        used = [0]

        def over_x2(rows, words):
            used[0] += words
            return x2[0:rows, used[0] - words:used[0]]

        posm = over_xp[:, NCH * LEAVES:(NCH + 2 * 7) * LEAVES].bitcast(F32).rearrange("p (t f) -> p t f", f=LEAVES)
        work = [over_x2(P, WCOLS + ROW) for i in range(NB)]
        xs = [wk[:, WCOLS:] for wk in work]
        os_ = [over_x2(P, CH) for i in range(NB)]
        xsT = [w2_f[0:WROWS, 0, i * P:(i + 1) * P].bitcast(F16).rearrange("r (a n) -> r a n", a=2)
               for i in range(NB)]
        wl = [[w2_p[0:WROWS, (2 * i + h) * LEVELS:(2 * i + h + 1) * LEVELS, :, :] for h in range(2)]
              for i in range(NB)]
        assert used[0] <= XCOLS
        ix = sb("ix", [P, NB], I32)

        banks = [ctx.enter_context(nc.psum_tensor(f"bank{i}", [P, 512], F32)) for i in range(8)]
        pre = [[banks[0], banks[1]], [banks[2], banks[3]]]
        p_fc, p_tr, p_sc, p_rk = banks[4], banks[5], banks[6], banks[7]
        p_conv = banks[0:2]
        p_x1T = [banks[2][:, :].bitcast(F16), banks[3][:, :].bitcast(F16)]
        p_xT = [banks[0][:, :].bitcast(F16), banks[1][:, :].bitcast(F16)]
        p_y = [banks[2], banks[3]]
        p_trh = p_tr[:, :].bitcast(F16)

        s_wc, s_wload, s_w1load, s_b2load, s_pool, s_trig, s_sin, s_wconv, s_xhi, s_xlo, s_whi = [sem(n) for n in (
            "wconv_loaded w_loaded w1_loaded b2_loaded pool_setup trig_ready "
            "sin_done wconv_ready x_high_ready x_low_ready weights_high_ready").split()]
        s_split, s_rows, s_w2s, s_w2p, s_b2p, s_fill, s_leafw = [sem(n) for n in (
            "split_done part_rows_moved w2_step w2_parts_ready b2_parts_ready slots_emptied leafw_filled").split()]
        s_conv, s_vare, s_srt, s_xpg, s_x1, s_tr1, s_hc = [sem(n) for n in (
            "conv_done var_eps_ready sqrt_ready group_parts_ready x1_ready group_transposed conv_rows_ready").split()]
        s_x = [sem(f"x_loaded{i}") for i in range(XQ)]
        s_mm = [sem(f"rec{l}_done") for l in range(2)]
        s_hi = [sem(f"h{l}_high_ready") for l in range(2)]
        s_lo = [sem(f"h{l}_low_ready") for l in range(2)]
        s_fc, s_h2, s_bn, s_stat, s_xp, s_xrow, s_xpT, s_xpTc, s_sc, s_scc = [sem(n) for n in (
            "fc_done h2_ready bn_ready stats_ready xp_ready xrow_ready xp_transposed xpT_copied scores_done "
            "scores_copied").split()]
        s_mask, s_m7, s_lev, s_plog, s_pw, s_pws, s_rk, s_rkc, s_rkm, s_cnt, s_rankt, s_rank = [sem(n) for n in (
            "masks_ready leaf_mask_ready level_scores plog_ready pw_ready pw_scaled rank_done rank_copied "
            "rkm_ready cnt_ready rank_t_ready rank_ready").split()]
        s_bias = sem("biases_added")
        s_norm_link, s_mask_link, s_dchain = sem("pool_norm_step"), sem("pool_mask_step"), sem("dve_step")
        s_cum, s_cumT, s_past, s_leafp, s_leaves, s_pos, s_scat = [sem(n) for n in (
            "cum_ready cumT_done past_ready winleaf_done leaves_ready pos_ready rows_scattered").split()]
        s_w2load = [sem(f"w2_loaded{i}") for i in range(2)]
        s_xs = [sem(f"xs{i}_loaded") for i in range(NB)]
        s_wl = [sem(f"wl{i}_loaded") for i in range(NB)]
        s_out = [sem(f"os{i}_stored") for i in range(NB)]
        s_xt, s_xtc, s_ixc, s_y, s_prod, s_o = [sem(n) for n in (
            "xsT_done xsT_copied ix_copied y_done prod_done o_ready").split()]
        s_passed = sem("passed")

        weights = (
            (wih0_hi[:, :], wih0_lo[0:CH, :], w_f32[:, 0, 0:H]),
            (w1_hi[:, :], w1_lo[0:CH, :], w1_f[:, :]),
            (b1_p[0:1, 0, :], b1_p[0:1, 1, :], b1_f[0:1, :]),
            (whh0_p[:, 0, :], whh0_p[:, 1, :], w_f32[:, 1, :]),
            (wih1_p[:, 0, :], wih1_p[:, 1, :], w_f32[:, 2, :]),
            (whh1_p[:, 0, :], whh1_p[:, 1, :], w_f32[:, 3, :]),
            (fc_p[:, 0, :], fc_p[:, 1, :], fc_f32[:, :, :].rearrange("p k c -> p (k c)")),
            (fcb_p[:, 0, :], fcb_p[:, 1, :], fcb_f32[0:1, :]),
            (bias_p[:, 0, :, :].rearrange("p l h -> p (l h)"), bias_p[:, 1, :, :].rearrange("p l h -> p (l h)"),
             bias_s[:, :, :].rearrange("p l h -> p (l h)")))

        block = ctx.enter_context(nc.Block())

        @block.sync
        def _(sp):
            sp.dma_start(ph[0:CH, :], phases[0:1, :].broadcast_to([CH, K // 2])).then_inc(s_wc, 16)
            sp.dma_start(ph[CH:P, :], phases[1:2, :].broadcast_to([CH, K // 2])).then_inc(s_wc, 16)
            sp.dma_start(wr[:, :, :], w_real).then_inc(s_wc, 16)
            sp.dma_start(wi[:, :, :], w_imag).then_inc(s_wc, 16)
            for i in range(XQ):
                part = slice(i * XCOLS // XQ, (i + 1) * XCOLS // XQ)
                sp.dma_start(x2[0:CH, part], xT[:, part]).then_inc(s_x[i], 16)
                sp.dma_start(x2[CH:P, part], xT[:, part.start + B:part.stop + B]).then_inc(s_x[i], 16)
            sp.dma_start(w_f32[0:CH, 0, 0:H], wih0).then_inc(s_wload, 16)
            sp.dma_start(w_f32[CH:P, 0, 0:H], wih0).then_inc(s_wload, 16)
            for n, w in ((1, whh0), (2, wih1), (3, whh1)):
                sp.dma_start(w_f32[:, n, :].rearrange("p (k h) -> p k h", k=KH),
                             w.rearrange("(k p) h -> p k h", p=P)).then_inc(s_wload, 16)
            sp.dma_start(fc_f32[:, :, :], fcw.rearrange("(k p) h -> p k h", p=P)).then_inc(s_wload, 16)
            for n, b in enumerate((bih0, bhh0, bih1, bhh1)):
                sp.dma_start(bias_f32[0:1, n, :], b).then_inc(s_wload, 16)
            sp.dma_start(fcb_f32[0:1, :], fcb).then_inc(s_wload, 16)
            for half in range(2):
                sp.dma_start(w1_f[half * CH:(half + 1) * CH, :], w1).then_inc(s_w1load, 16)
            sp.dma_start(b1_f[0:1, :], b1).then_inc(s_w1load, 16)
            sp.dma_start(b2_f[0:INNER, 0, :], b2[0:INNER, :]).then_inc(s_b2load, 16)
            sp.dma_start(b2_f[:, 1, :], b2[INNER:, :]).then_inc(s_b2load, 16)
            def path_matrices(g):
                n = LEAVES // WQ
                if g >= 2:
                    sp.wait_ge(s_w2p, g - 1)
                up = min(n, INNER - g * n)
                dst = w2_f[:, g % 2, :].rearrange("p (n o) -> p n o", o=CH)
                sp.dma_start(dst[0:CH, 0:up, :],
                             w2[g * n:g * n + up, :, :].rearrange("n d o -> d n o")).then_inc(s_w2load[g % 2], 16)
                sp.dma_start(dst[CH:P, :, :],
                             w2[INNER + g * n:INNER + (g + 1) * n, :, :].rearrange("n d o -> d n o")).then_inc(s_w2load[g % 2], 16)

            path_matrices(0)
            path_matrices(1)
            sp.wait_ge(s_split, 1)
            for p in range(2):
                sp.dma_start(wih0_lo[CH + p:CH + p + 1, :], bias_p[0:1, p, 0, :]).then_inc(s_rows, 16)
                sp.dma_start(bias1_2[p:p + 1, :], bias_p[0:1, p, 1, :]).then_inc(s_rows, 16)
                sp.dma_start(fcb_2[p:p + 1, :], fcb_p[0:1, p, :]).then_inc(s_rows, 16)
                sp.dma_start(w1_lo[CH + p:CH + p + 1, :], b1_p[0:1, p, :]).then_inc(s_rows, 16)
            for g in range(2, WQ):
                path_matrices(g)
            sp.wait_ge(s_pool, N_POOL_SETUP)
            sp.dma_start(sorted_in.rearrange("(w p) c -> p w c", p=P),
                         empty[:, :].unsqueeze(1).broadcast_to([P, NPAIR, ROW])).then_inc(s_fill, 16)
            sp.wait_ge(s_w2p, WQ)
            sp.wait_ge(s_b2p, 1)
            table = w_leaf.rearrange("(f r) c -> r f c", r=WROWS)
            for l in range(LEVELS):
                last = l == LEVELS - 1
                n0, n, rep = (0 if last else 2 ** l - 1), 2 ** l, LEAVES >> l
                cols = slice(l * 2 * CH, (l + 1) * 2 * CH)
                rows = slice(CH, P) if last else slice(0, CH)
                level = w2_p[rows, n0:n0 + n, :, :].rearrange("d n a o -> d n (a o)")
                if n < rep:
                    for m in range(n):
                        sp.dma_start(table[0:CH, m * rep:(m + 1) * rep, cols],
                                     level[:, m:m + 1, :].broadcast_to([CH, rep, 2 * CH])).then_inc(s_leafw, 16)
                else:
                    for m in range(rep):
                        sp.dma_start(table[0:CH, m::rep, cols], level).then_inc(s_leafw, 16)
                sp.dma_start(table[CH, :, cols].rearrange("(n r) c -> n r c", r=rep),
                             b2_p[n0:n0 + n, int(last), :, :].rearrange("n a o -> n (a o)").unsqueeze(1)
                             .broadcast_to([n, rep, 2 * CH])).then_inc(s_leafw, 16)

            sp.wait_ge(s_leafw, 16 * N_TABLE_DMAS)
            sp.wait_ge(s_leaves, 1)

            loaded = [None]

            def matrices(w, b, uses):
                if is_known(w, 0):
                    leaves = sp.value_load(pair_leaves[0:1, 0:1])
                elif b % 2:
                    loaded[0] = sp.value_load(four_leaves[0:1, bass.ds(NB // 2 * uses + (b - 1) // 2, 1)])
                    leaves = loaded[0] % LEAVES ** 2
                else:
                    leaves = loaded[0] // LEAVES ** 2
                if not is_known(uses, 0):
                    sp.wait_ge(s_y, w - NB + 1)
                for h, leaf in enumerate((leaves % LEAVES, leaves // LEAVES)):
                    sp.dma_start(wl[b][h].rearrange("r l a o -> r (l a o)"),
                                 w_leaf[bass.ds(leaf * WROWS, WROWS), :]).then_inc(s_wl[b], 16)

            def load(w, b, uses):
                if not is_known(uses, 0):
                    matrices(w, b, uses)

            for b in range(NB):
                matrices(b, b, 0)
            run_pairs(sp, load)

        @block.gpsimd
        def _(pool):
            done = [0]

            def setup(ins):
                done[0] += 1
                ins.then_inc(s_pool, 1)
                pool.wait_ge(s_pool, done[0])

            setup(pool.memset(ident_h[:, :], 0.0))
            setup(pool.affine_select(out=ident_h[:, :], in_=ident_h[:, :], compare_op=ALU.not_equal, fill=1.0,
                                     base=0, pattern=[[-1, P]], channel_multiplier=1))
            setup(pool.memset(x_p[:, :, XCOLS:], 0.0))
            setup(pool.memset(x1b[CH:CH + 2, :], 1.0))
            setup(pool.memset(xbT[:, :], 0.0))
            setup(pool.memset(xbT[CH:CH + 2, :], 1.0))
            setup(pool.memset(xpT[:, TT:], 0.0))
            for h in (h_hi[1], h_lo[1]):
                setup(pool.memset(h[:, :, :, TT:], 0.0))
            setup(pool.memset(ones_2[:, :], 1.0))
            setup(pool.memset(ones_f[:, :], 1.0))
            setup(pool.memset(ones_bf[:, :], 1.0))
            setup(pool.memset(before[:, :], 0.0))
            setup(pool.affine_select(out=before[:, :], in_=before[:, :], compare_op=ALU.is_ge, fill=1.0,
                                     base=0, pattern=[[-1, P]], channel_multiplier=1))
            setup(pool.memset(first_p[:, :], 0.0))
            setup(pool.affine_select(out=first_p[:, :], in_=first_p[:, :], compare_op=ALU.not_equal, fill=1.0,
                                     base=0, pattern=[[-1, 1]], channel_multiplier=1))
            setup(pool.memset(eps_t[:, :], EPS))
            setup(pool.memset(mhalf[:, :], -0.5))
            setup(pool.memset(descale[:, :], 1 / WSCALE))
            setup(pool.memset(empty[:, :], 0.0))
            setup(pool.memset(empty[:, IDX:IDX + 1].bitcast(I32), NOBODY))
            setup(pool.memset(cnt[:, :], 0.0))
            for q in range(2):
                setup(pool.memset(mask[q][:, 0:1], 1.0))
            setup(pool.iota(win_no[:, :], pattern=[[1, NWIN]], base=0, channel_multiplier=0,
                            allow_small_or_imprecise_dtypes=True))
            setup(pool.iota(xrow[:, :, IDX:IDX + 1].bitcast(I32), pattern=[[TT, NCH], [1, 1]], base=0,
                            channel_multiplier=1))
            assert done[0] == N_POOL_SETUP, done[0]
            step = [0]

            def link(ins):
                step[0] += 1
                ins.then_inc(s_w2s, 1)
                pool.wait_ge(s_w2s, step[0])

            pool.wait_ge(s_b2load, 32)
            for half, rows in ((0, slice(0, INNER)), (1, slice(0, P))):
                link(pool.tensor_scalar(b2_f[rows, half, :], b2_f[rows, half, :], WSCALE, None, ALU.mult))
                link(pool.tensor_copy(b2_p[rows, half, 0, :], b2_f[rows, half, :]))
                last = pool.tensor_tensor(b2_p[rows, half, 1, :], b2_f[rows, half, :], b2_p[rows, half, 0, :],
                                          ALU.subtract)
                if half == 0:
                    link(last)
            last.then_inc(s_b2p, 1)
            pool.wait_ge(s_b2p, 1)
            n = LEAVES // WQ
            for g in range(WQ):
                pool.wait_ge(s_w2load[g % 2], 32 * (g // 2 + 1))
                parts = [(P, n)] if g < WQ - 1 else [(P, n - 1), (None, 1)]
                for m, (rows_n, k) in enumerate(parts):
                    rows = slice(0, P) if rows_n else slice(CH, P)
                    k0 = 0 if rows_n else n - 1
                    src = w2_f[rows, g % 2, k0 * CH:(k0 + k) * CH].rearrange("p (n o) -> p n o", o=CH)
                    dst = w2_p[rows, g * n + k0:g * n + k0 + k, :, :]
                    link(pool.tensor_scalar(src, src, WSCALE, None, ALU.mult))
                    link(pool.tensor_copy(dst[:, :, 0, :], src))
                    last = pool.tensor_tensor(dst[:, :, 1, :], src, dst[:, :, 0, :], ALU.subtract)
                    if m < len(parts) - 1:
                        link(last)
                last.then_inc(s_w2p, 1)
                pool.wait_ge(s_w2p, g + 1)

            def norm(t, q):
                step = [0]

                def link(ins):
                    step[0] += 1
                    ins.then_inc(s_norm_link, 1)
                    pool.wait_ge(s_norm_link, t * NORM_LINKS + step[0])

                pool.wait_ge(s_stat, t + 1)
                link(pool.tensor_tensor(rs2[:, :], mv[:, 1:2], eps_t[:, :], ALU.add))
                link(pool.tensor_tensor(rs2[:, :], rs2[:, :], mhalf[:, :], ALU.pow))
                link(pool.tensor_tensor(d2[:, :], tile_of(t, xrow)[:, RES:XP], mv[:, 0:1].broadcast_to([TT, CH]),
                                        ALU.subtract))
                link(pool.tensor_tensor(xn[:, :], d2[:, :], rs2[:, :].broadcast_to([TT, CH]), ALU.mult))
                pool.sem_inc(s_passed, 1)
                pool.tensor_copy(xp[:, 0, :], xn[:, :]).then_inc(s_xp, 1)
                pool.wait_ge(s_xp, 2 * t + 1)
                pool.tensor_tensor(xp[:, 1, :], xn[:, :], xp[:, 0, :], ALU.subtract).then_inc(s_xp, 1)
                pool.wait_ge(s_xp, 2 * t + 2)
                pool.sem_inc(s_passed, 1)
                pool.tensor_copy(tile_of(t, xrow)[:, XP:PW].bitcast(F16),
                                 xp[:, :, :].rearrange("p a c -> p (a c)")).then_inc(s_xrow, 1)
                assert step[0] == NORM_LINKS

            def masks(t, q):
                step = [0]

                def link(ins):
                    step[0] += 1
                    ins.then_inc(s_mask_link, 1)
                    pool.wait_ge(s_mask_link, t * MASK_LINKS + step[0])

                pool.wait_ge(s_scc, t + 1)
                pool.sem_inc(s_passed, 1)
                link(pool.tensor_scalar(right[:, :], sc[q][:, 0:INNER], 0.0, None, ALU.is_gt))
                for l in range(LEVELS - 1):
                    a, n = 2 ** l - 1, 2 ** l
                    kids = mask[q][:, 2 * n - 1:4 * n - 1].rearrange("p (n t) -> p n t", t=2)
                    yes = pool.tensor_tensor(kids[:, :, 1], mask[q][:, a:a + n], right[:, a:a + n], ALU.mult)
                    link(yes)
                    no = pool.tensor_tensor(kids[:, :, 0], mask[q][:, a:a + n], kids[:, :, 1], ALU.subtract)
                    if l < LEVELS - 3:
                        link(no)
                    else:
                        no.then_inc(s_mask, 1)
                        if l == LEVELS - 3:
                            pool.wait_ge(s_mask, 2 * t + 1)
                pool.wait_ge(s_mask, 2 * t + 2)
                pool.tensor_copy(tile_of(t, mask_bf), mask[q][:, INNER:NODES]).then_inc(s_m7, 1)
                assert step[0] == MASK_LINKS, step[0]

            def ranks(t, q):
                pool.wait_ge(s_rkc, t + 1)
                if not (isinstance(t, int) and t == 0):
                    pool.wait_ge(s_rank, t)
                pool.tensor_tensor(rkm[:, :], rk[0:TT, 0, :], cnt[0:TT, :], ALU.add).then_inc(s_rkm, 1)
                pool.wait_ge(s_rkm, t + 1)
                pool.tensor_tensor(cnt[:, :], cnt[:, :], rk[:, 1, :], ALU.add).then_inc(s_cnt, 1)
                pool.wait_ge(s_cnt, t + 1)

            def chunk(c, q, on):
                if on["norm"]:
                    norm(c - 4, q)
                if on["path"]:
                    ranks(c - 5, 1 - q)
                if on["norm"] and on["rec1"]:
                    masks(c - 4, q)

            pool.wait_ge(s_x1, GROUPS)
            run_chunks(pool, chunk)

            for i in range(NB):
                pool.memset(xsT[i][CH:WROWS, 0, :], 1.0).then_inc(s_pool, 1)
            pool.wait_ge(s_pool, N_POOL_SETUP + NB)
            pool.wait_ge(s_fill, 16)
            pool.wait_ge(s_pws, NCH)
            pool.wait_ge(s_xrow, NCH)
            for t in range(NCH):
                if t % 7 == 0:
                    pool.wait_ge(s_pos, t // 7 + 1)
                pool.indirect_dma_start(sorted_in, bass.IndirectOffsetOnAxis(ap=pos[:, t:t + 1], axis=0),
                                        xrow[:, t, :], None).then_inc(s_scat, 16)

            def store(w, b, uses):
                pool.wait_ge(s_ixc, w + 1)
                pool.wait_ge(s_o, w + 1)
                pool.sem_inc(s_passed, 1)
                pool.indirect_dma_start(out, bass.IndirectOffsetOnAxis(ap=ix[:, b:b + 1], axis=0), os_[b], None,
                                        bounds_check=NT - 1, oob_is_err=False).then_inc(s_out[b], 16)

            run_pairs(pool, store)
            for b in range(NB):
                pool.wait_ge(s_out[b], 16 * len(range(b, NPAIR, NB)))

        @block.vector
        def _(dve):
            v = nc.vector
            chain = [0]

            def link(ins):
                chain[0] += 1
                ins.then_inc(s_dchain, 1)
                dve.wait_ge(s_dchain, chain[0])

            dve.wait_ge(s_wc, 64)
            link(v.tensor_scalar(trig[:, 0, :], ph[:, :], PI / 2, None, ALU.add))
            link(v.tensor_copy(trig[:, 1, :], ph[:, :]))
            link(v.tensor_scalar(turns[:, :, :], trig[:, :, :], 1 / (2 * PI), ROUND, ALU.mult, ALU.add))
            link(v.tensor_scalar(turns[:, :, :], turns[:, :, :], ROUND, None, ALU.subtract))
            link(v.scalar_tensor_tensor(trig[:, :, :], turns[:, :, :], -TWO_PI_HIGH, trig[:, :, :],
                                        ALU.mult, ALU.add))
            link(v.scalar_tensor_tensor(trig[:, :, :], turns[:, :, :], -TWO_PI_LOW, trig[:, :, :],
                                        ALU.mult, ALU.add))
            v.tensor_scalar(trig[:, :, :], trig[:, :, :], 3.1415925, -3.1415925, ALU.min, ALU.max).then_inc(s_trig, 1)
            dve.wait_ge(s_sin, 1)
            for k in range(K // 2):
                imag = v.tensor_scalar(wtmp[:, k, :], wi[:, k, :], trig[:, 1, k:k + 1], None, ALU.mult)
            link(imag)
            for k in range(K // 2):
                real = v.scalar_tensor_tensor(wc[:, k, :], wr[:, k, :], trig[:, 0, k:k + 1], wtmp[:, k, :],
                                              ALU.mult, ALU.subtract)
            link(real)
            link(v.tensor_scalar(wc_p[:, :, 0, :], wc[:, :, :], WSCALE, None, ALU.mult))
            v.scalar_tensor_tensor(wc_p[:, :, 1, :], wc[:, :, :], WSCALE, wc_p[:, :, 0, :],
                                   ALU.mult, ALU.subtract).then_inc(s_wconv, 1)
            for i in range(XQ):
                part = slice(i * XCOLS // XQ, (i + 1) * XCOLS // XQ)
                dve.wait_ge(s_xhi, i + 1)
                v.tensor_tensor(x_p[:, 1, part], x2[:, part], x_p[:, 0, part], ALU.subtract).then_inc(s_xlo, 1)
            dve.wait_ge(s_wload, 16 * 11)
            dve.wait_ge(s_w1load, 48)
            link(v.tensor_tensor(bias_s[0:1, 0, :], bias_f32[0:1, 0, :], bias_f32[0:1, 1, :], ALU.add))
            v.tensor_tensor(bias_s[0:1, 1, :], bias_f32[0:1, 2, :], bias_f32[0:1, 3, :], ALU.add).then_inc(s_bias, 1)

            def stats(g):
                dve.wait_ge(s_hc, g + 1)
                for i in range(GT):
                    last = v.bn_stats(stg[:, i, :], xrow[:, GT * g + i, RES:XP])
                link(last)

            stats(0)
            for g in range(GROUPS):
                rows = xrow[:, GT * g:GT * (g + 1), RES:XP]
                for i in range(GT):
                    last = v.bn_aggr(mvg[:, i, :], stg[:, i, :])
                link(last)
                v.tensor_scalar(var[:, :], mvg[:, :, 1], EPS, None, ALU.add).then_inc(s_vare, 1)
                link(v.tensor_tensor(xng[:, :, :], rows, mvg[:, :, 0:1].broadcast_to([TT, GT, CH]), ALU.subtract))
                if g + 1 < GROUPS:
                    stats(g + 1)
                dve.wait_ge(s_srt, g + 1)
                link(v.reciprocal(rcp[:, :], srt[:, :]))
                link(v.scalar_tensor_tensor(newton[:, :], rcp[:, :], -0.5, var[:, :], ALU.mult, ALU.mult))
                link(v.tensor_tensor(newton[:, :], newton[:, :], rcp[:, :], ALU.mult))
                link(v.scalar_tensor_tensor(rcp[:, :], newton[:, :], 1.5, rcp[:, :], ALU.add, ALU.mult))
                link(v.tensor_tensor(xng[:, :, :], xng[:, :, :], rcp[:, :].unsqueeze(2).broadcast_to([TT, GT, CH]),
                                     ALU.mult))
                if g >= 2:
                    dve.wait_ge(s_tr1, g - 1)
                link(v.tensor_copy(xpg[:, g % 2, :, 0, :], xng[:, :, :]))
                v.tensor_tensor(xpg[:, g % 2, :, 1, :], xng[:, :, :], xpg[:, g % 2, :, 0, :],
                                ALU.subtract).then_inc(s_xpg, 1)
                if g == 0:
                    for n, (hi, lo, full) in enumerate(weights):
                        dve.wait_ge(s_whi, n + 1)
                        lo = v.scalar_tensor_tensor(lo, full[0:lo.shape[0]], WSCALE, hi[0:lo.shape[0]], ALU.mult, ALU.subtract)
                    lo.then_inc(s_split, 1)

            def low(l, c, k, q):
                dve.wait_ge(s_hi[l], c * C + k + 1)
                col = slice(k * B, (k + 1) * B)
                v.tensor_tensor(h_lo[l][:, q, :, col], h_f[l][:, :, :], h_hi[l][:, q, :, col],
                                ALU.subtract).then_inc(s_lo[l], 1)

            def norm(k, t, q):
                if k == 0:
                    dve.wait_ge(s_fc, t + 1)
                    row = tile_of(t, xrow)[:, RES:XP]
                    v.scalar_tensor_tensor(row, p_fc[0:TT, 0:CH], 1 / WSCALE, row, ALU.mult, ALU.add).then_inc(s_h2, 1)
                elif k == 1:
                    dve.wait_ge(s_h2, t + 1)
                    dve.sem_inc(s_passed, 1)
                    v.bn_stats(st[:, :], tile_of(t, xrow)[:, RES:XP]).then_inc(s_bn, 1)
                elif k == 2:
                    dve.wait_ge(s_bn, t + 1)
                    if not (isinstance(t, int) and t == 0):
                        dve.wait_ge(s_xp, 2 * t)
                    dve.sem_inc(s_passed, 1)
                    v.bn_aggr(mv[:, :], st[:, :]).then_inc(s_stat, 1)

            def path(k, t, q):
                l = k - 4
                if 0 <= l < LEVELS:
                    if l == 0:
                        dve.wait_ge(s_mask, 2 * t + 2)
                        if not (isinstance(t, int) and t == 0):
                            dve.wait_ge(s_pw, t)
                    nodes = slice(2 ** l - 1, 2 ** (l + 1) - 1)
                    v.tensor_tensor_reduce(out=picked[:, nodes], in0=mask[q][:, nodes], in1=sc[q][:, nodes],
                                           scale=1.0, scalar=0.0, op0=ALU.mult, op1=ALU.add,
                                           accum_out=plog[:, l:l + 1]).then_inc(s_lev, 1)
                elif k == 12:
                    dve.wait_ge(s_lev, t * LEVELS + LEVELS)
                    v.scalar_tensor_tensor(plog[:, :], plog[:, :], -1.0, plog[:, :], ALU.mult, ALU.max).then_inc(s_plog, 1)
                elif k == 13:
                    dve.wait_ge(s_rkm, t + 1)
                    v.tensor_tensor_reduce(out=rkr[:, :], in0=rkm[:, :], in1=mask[q][:, INNER:NODES], scale=1.0,
                                           scalar=0.0, op0=ALU.mult, op1=ALU.add,
                                           accum_out=rank_t[:, :]).then_inc(s_rankt, 1)
                elif k == 14:
                    dve.wait_ge(s_rankt, t + 1)
                    v.tensor_tensor(rank[:, bass.ds(t, 1)], rank_t[:, :], rank_t[:, :], ALU.max).then_inc(s_rank, 1)
                    dve.wait_ge(s_pw, t + 1)
                    v.tensor_tensor(tile_of(t, xrow)[:, PW:IDX], pws[:, :], descale[:, :], ALU.mult).then_inc(s_pws, 1)

            def masks(t, q):
                dve.wait_ge(s_scc, t + 1)
                dve.wait_ge(s_m7, t)
                link(v.tensor_scalar(right[:, :], sc[q][:, 0:INNER], 0.0, None, ALU.is_gt))
                for l in range(LEVELS - 1):
                    a, n = 2 ** l - 1, 2 ** l
                    kids = mask[q][:, 2 * n - 1:4 * n - 1].rearrange("p (n t) -> p n t", t=2)
                    link(v.tensor_tensor(kids[:, :, 1], mask[q][:, a:a + n], right[:, a:a + n], ALU.mult))
                    link(v.tensor_tensor(kids[:, :, 0], mask[q][:, a:a + n], kids[:, :, 1], ALU.subtract))
                v.tensor_copy(tile_of(t, mask_bf), mask[q][:, INNER:NODES]).then_inc(s_m7, 1)
                dve.sem_inc(s_mask, 2)

            def chunk(c, q, on):
                for k in range(C):
                    if on["rec0"]:
                        low(0, c, k, q)
                    if on["norm"]:
                        norm(k, c - 4, q)
                    if on["rec1"]:
                        low(1, c - 2, k, q)
                    if on["path"]:
                        path(k, c - 5, 1 - q)
                if on["norm"] and not on["rec1"]:
                    masks(c - 4, q)

            run_chunks(dve, chunk)

            dve.wait_ge(s_cnt, NCH)
            link(v.tensor_scalar(wins[:, :], cnt[:, :], float(WIN - 1), None, ALU.add))
            link(v.tensor_copy(cnt_i, wins[:, :]))
            link(v.tensor_scalar(cnt_i, cnt_i, WIN.bit_length() - 1, None, ALU.arith_shift_right))
            link(v.tensor_copy(wins[:, :], cnt_i))
            link(v.tensor_copy(cums[:, 0, :], wins[:, :]))
            a, d = 0, 1
            while d < LEAVES:
                v.tensor_copy(cums[:, 1 - a, 0:d], cums[:, a, 0:d])
                link(v.tensor_tensor(cums[:, 1 - a, d:], cums[:, a, d:], cums[:, a, 0:LEAVES - d], ALU.add))
                a, d = 1 - a, 2 * d
            v.tensor_tensor(base, cums[:, a, :], wins[:, :], ALU.subtract).then_inc(s_cum, 1)
            dve.wait_ge(s_cum, 1)
            link(v.tensor_scalar(base, base, float(WIN), None, ALU.mult))
            def slots(g):
                tiles = slice(7 * g, 7 * g + 7)
                link(v.tensor_tensor(posm[:, :, :], mask_bf[:, tiles, :],
                                     base[0:TT, :].unsqueeze(1).broadcast_to([TT, 7, LEAVES]), ALU.mult))
                link(v.tensor_reduce(posb[:, tiles], posm[:, :, :], AX.X, ALU.add))
                v.tensor_tensor(pos[:, tiles], posb[:, tiles], rank[:, tiles], ALU.add).then_inc(s_pos, 1)

            slots(0)
            dve.wait_ge(s_cumT, 1)
            link(v.tensor_copy(cumT[:, :], p_tr[:, 0:1]))
            v.tensor_scalar(past, win_no[:, :], cumT[:, 0:1], None, ALU.is_ge).then_inc(s_past, 1)
            dve.wait_ge(s_leafp, 1)
            link(v.tensor_scalar(leaf_of[0:1, :, :].rearrange("p w h -> p (w h)"), p_sc[0:1, 0:NWIN],
                                 float(LEAVES - 1), None, ALU.min))
            link(v.scalar_tensor_tensor(pair_leaves[0:1, :], leaf_of[0:1, :, 1], float(LEAVES), leaf_of[0:1, :, 0],
                                        ALU.mult, ALU.add))
            link(v.tensor_scalar(four_leaves, pair_leaves[0:1, 2::2], 14, None, ALU.logical_shift_left))
            v.tensor_tensor(four_leaves, four_leaves, pair_leaves[0:1, 1::2], ALU.bitwise_or).then_inc(s_leaves, 1)
            for g in range(1, NCH // 7):
                slots(g)

            def weigh(w, b, uses):
                dve.wait_ge(s_y, w + 1)
                dve.wait_ge(s_xs[b], uses * 16 + 16)
                v.tensor_tensor(work[b][:, 0:WCOLS].rearrange("p (l o) -> p l o", l=LEVELS),
                                p_y[b % 2][:, :].rearrange("p (l o) -> p l o", l=LEVELS),
                                xs[b][:, PW:IDX].unsqueeze(2).broadcast_to([P, LEVELS, CH]),
                                ALU.mult).then_inc(s_prod, 1)

            def pair(w, b, uses):
                if not is_known(w, NPAIR - 1):
                    weigh(w + 1, (b + 1) % NB, uses + (b + 1) // NB)
                dve.wait_ge(s_prod, w + 1)
                if not is_known(uses, 0):
                    dve.wait_ge(s_out[b], uses * 16)
                v.tensor_reduce(os_[b], work[b][:, 0:WCOLS + CH].rearrange("p (l o) -> p o l", l=LEVELS + 1),
                                AX.X, ALU.add).then_inc(s_o, 1)

            weigh(0, 0, 0)
            run_pairs(dve, pair)

        @block.scalar
        def _(act):
            a = nc.scalar
            act.wait_ge(s_trig, 1)
            a.activation(trig[:, :, :], trig[:, :, :], ACT.Sin).then_inc(s_sin, 1)
            a.preload_act_table_set("sqrt_and_others")

            for i in range(XQ):
                part = slice(i * XCOLS // XQ, (i + 1) * XCOLS // XQ)
                act.wait_ge(s_x[i], 32)
                a.activation(x_p[:, 0, part], x2[:, part], ACT.Copy).then_inc(s_xhi, 1)
            act.wait_ge(s_wload, 16 * 11)
            act.wait_ge(s_w1load, 48)
            act.wait_ge(s_bias, 1)
            for hi, lo, full in weights:
                a.activation(hi, full, ACT.Copy, scale=WSCALE).then_inc(s_whi, 1)

            def copy_conv(g):
                act.wait_ge(s_conv, GT * (g + 1))
                a.activation(xrow[:, GT * g:GT * (g + 1), RES:XP],
                             p_conv[g % 2][0:TT, 0:GT * CH].rearrange("p (g c) -> p g c", c=CH),
                             ACT.Copy, scale=1 / WSCALE).then_inc(s_hc, 1)

            def copy_x1(g):
                act.wait_ge(s_tr1, g + 1)
                tok = slice(g * GT * TT, (g + 1) * GT * TT)
                a.activation(x1b[0:CH, tok], p_x1T[g % 2][0:CH, 0:GT * TT], ACT.Copy)
                a.activation(x1s[:, tok], p_x1T[g % 2][:, 0:GT * TT], ACT.Copy).then_inc(s_x1, 1)

            copy_conv(0)
            for g in range(GROUPS):
                if g + 1 < GROUPS:
                    copy_conv(g + 1)
                act.wait_ge(s_vare, g + 1)
                a.activation(srt[:, :], var[:, :], ACT.Sqrt).then_inc(s_srt, 1)
                if g:
                    copy_x1(g - 1)
            copy_x1(GROUPS - 1)
            a.preload_act_table_set("gelu_and_others")

            def tanh(l, c, k, q):
                act.wait_ge(s_mm[l], c * C + k + 1)
                col = slice(k * B, (k + 1) * B)
                z = pre[l][q][:, 0:MH * TT].rearrange("p (m n) -> p m n", m=MH)[:, :, col]
                a.activation(h_f[l][:, :, :], z, ACT.Tanh, scale=1 / WSCALE)
                a.activation(h_hi[l][:, q, :, col], z, ACT.Tanh, scale=1 / WSCALE).then_inc(s_hi[l], 1)

            def norm(k, t, q):
                if k == 7:
                    act.wait_ge(s_xpT, t + 1)
                    a.activation(xbT[0:CH, 0:TT], p_trh[0:CH, 0:TT], ACT.Copy)
                    a.activation(xpT[:, 0:TT], p_trh[:, 0:TT], ACT.Copy).then_inc(s_xpTc, 1)
                elif k == 10:
                    act.wait_ge(s_sc, t + 1)
                    a.activation(sc[q][:, :], p_sc[0:TT, 0:NODES], ACT.Copy).then_inc(s_scc, 1)

            def path(k, t, q):
                if k == 6:
                    act.wait_ge(s_rk, t + 1)
                    if not is_known(t, 0):
                        act.wait_ge(s_cnt, t)
                    a.activation(rk[:, :, :].rearrange("p a c -> p (a c)"), p_rk[:, 0:2 * LEAVES],
                                 ACT.Copy).then_inc(s_rkc, 1)
                elif k == 13:
                    act.wait_ge(s_plog, t + 1)
                    if not (isinstance(t, int) and t == 0):
                        act.wait_ge(s_pws, t)
                    a.activation(pws[:, :], plog[:, :], ACT.Gelu, scale=1 / WSCALE).then_inc(s_pw, 1)

            def chunk(c, q, on):
                for k in range(C):
                    if on["rec0"]:
                        tanh(0, c, k, q)
                    if on["path"]:
                        path(k, c - 5, 1 - q)
                    if on["rec1"]:
                        tanh(1, c - 2, k, q)
                    if on["norm"]:
                        norm(k, c - 4, q)

            run_chunks(act, chunk)

            def rows(w, b):
                act.dma_start(xs[b], sorted_in[bass.ds(w * P, P), :]).then_inc(s_xs[b], 16)

            def pair(w, b, uses):
                act.wait_ge(s_xt, w + 1)
                if not is_known(uses, 0):
                    act.wait_ge(s_y, w - NB + 1)
                a.activation(xsT[b][0:CH, 0, :], p_xT[b % 2][0:CH, 0:P], ACT.Copy)
                a.activation(xsT[b][0:CH, 1, :], p_xT[b % 2][CH:P, 0:P], ACT.Copy).then_inc(s_xtc, 1)
                if not is_known(uses, 0):
                    act.wait_ge(s_out[b], uses * 16)
                a.activation(ix[:, b:b + 1], xs[b][:, IDX:IDX + 1].bitcast(I32), ACT.Copy).then_inc(s_ixc, 1)
                if isinstance(w, int) and w + AHEAD >= NPAIR:
                    return
                if not (isinstance(w, int) and w + AHEAD < NB):
                    act.wait_ge(s_o, w + AHEAD - NB + 1)
                    act.wait_ge(s_ixc, w + AHEAD - NB + 1)
                rows(w + AHEAD, (b + AHEAD) % NB)

            act.wait_ge(s_scat, 16 * NCH)
            for b in range(AHEAD):
                rows(b, b)
            run_pairs(act, pair)

        @block.tensor
        def _(pe):
            mm = nc.tensor.matmul
            pe.wait_ge(s_wconv, 1)
            pe.wait_ge(s_pool, 3)

            def conv(g):
                end = (g + 1) * GT * TT + (K - 2) * B
                pe.wait_ge(s_xlo, -(-end * XQ // XCOLS))
                if g >= 2:
                    pe.wait_ge(s_hc, g - 1)
                for i in range(GT):
                    z = p_conv[g % 2][:, i * CH:(i + 1) * CH]
                    for k in range(K // 2):
                        at = (g * GT + i) * TT + 2 * k * B
                        cols = slice(at, at + P)
                        mm(z, x_p[:, 0, cols], wc_p[:, k, 0, :], start=(k == 0), stop=False)
                        mm(z, x_p[:, 0, cols], wc_p[:, k, 1, :], start=False, stop=False)
                        last = mm(z, x_p[:, 1, cols], wc_p[:, k, 0, :], start=False, stop=(k == K // 2 - 1))
                    last.then_inc(s_conv, 1)

            conv(0)
            conv(1)
            for g in range(GROUPS):
                if g + 2 < GROUPS:
                    conv(g + 2)
                pe.wait_ge(s_xpg, g + 1)
                if g >= 2:
                    pe.wait_ge(s_x1, g - 1)
                for i in range(GT):
                    last = nc.tensor.transpose(p_x1T[g % 2][:, i * TT:(i + 1) * TT],
                                               xpg[:, g % 2, i, :, :].rearrange("p a c -> p (a c)"),
                                               ident_h[0:TT, 0:TT])
                last.then_inc(s_tr1, 1)

            def shared(z, w, x, start=False):
                return mm(z, w, x, start=start, stop=True, skip_group_check=True)

            def in0(n, q, piece):
                m, j = divmod(piece, 2)
                z, ms = pre[0][q][:, m * TT:(m + 1) * TT], slice(m * P, (m + 1) * P)
                cols = bass.ds(n * TT, TT)
                if j == 0:
                    shared(z, wih0_hi[:, ms], x1s[:, cols], start=(piece == 0))
                else:
                    last = shared(z, wih0_lo[:, ms], x1b[:, cols])
                    if m == MH - 1 and isinstance(n, int) and n == 0:
                        last.then_inc(s_mm[0], 1)

            def in1(n, q, piece):
                m, j = divmod(piece, 7)
                z, ms = pre[1][q][:, m * TT:(m + 1) * TT], slice(m * P, (m + 1) * P)
                if j < 6:
                    k, (p, h) = j // 3, ((0, h_hi), (0, h_lo), (1, h_hi))[j % 3]
                    shared(z, wih1_p[:, p, k * H + m * P:k * H + (m + 1) * P], h[0][:, q, k, 0:TT],
                           start=(piece == 0))
                else:
                    last = shared(z, bias1_2[:, ms], ones_2[:, 0:TT])
                    if m == MH - 1 and isinstance(n, int) and n == 0:
                        last.then_inc(s_mm[1], 1)

            def fc(t, q, piece):
                z = p_fc[:, 0:CH]
                if piece == 0 and not (isinstance(t, int) and t == 0):
                    pe.wait_ge(s_h2, t)
                if piece < 6:
                    k, (p, h) = piece // 3, ((0, h_hi), (0, h_lo), (1, h_hi))[piece % 3]
                    mm(z, h[1][:, q, k, :], fc_p[:, p, k * CH:(k + 1) * CH], start=(piece == 0), stop=False)
                else:
                    mm(z, ones_2[:, :], fcb_2[:, :], start=False, stop=True).then_inc(s_fc, 1)

            def turn(t):
                pe.wait_ge(s_xp, 2 * t + 2)
                nc.tensor.transpose(p_trh[:, 0:TT], xp[:, :, :].rearrange("p a c -> p (a c)"),
                                    ident_h[0:TT, 0:TT]).then_inc(s_xpT, 1)

            def scores(t, piece):
                half, part = divmod(piece, 2)
                nodes = slice(half * P, min((half + 1) * P, NODES))
                if part == 0:
                    if piece == 0:
                        pe.wait_ge(s_xpTc, t + 1)
                    mm(p_sc[:, nodes], xpT[:, :], w1_hi[:, nodes], start=True, stop=False)
                else:
                    last = mm(p_sc[:, nodes], xbT[:, :], w1_lo[:, nodes], start=False, stop=True)
                    if half:
                        last.then_inc(s_sc, 1)

            def ranks(t, piece):
                m7 = tile_of(t, mask_bf)
                if piece == 0:
                    pe.wait_ge(s_m7, t + 1)
                    mm(p_rk[:, 0:LEAVES], before[:, :], m7, start=True, stop=True)
                else:
                    mm(p_rk[:, LEAVES:2 * LEAVES], ones_bf[:, :], m7, start=True, stop=True).then_inc(s_rk, 1)

            def side(n, c, q, on):
                if n < 4:
                    if on["in0"]:
                        in0(c + 1, 1 - q, n)
                elif n in (9, 11):
                    if on["path"]:
                        ranks(c - 5, (n - 9) // 2)
                elif n == 12:
                    if on["norm"]:
                        turn(c - 4)
                elif 16 <= n < 20:
                    if on["norm"]:
                        scores(c - 4, n - 16)
                elif n < 25:
                    if on["in1"]:
                        in1(c - 1, 1 - q, n - 4 - (n > 9) - (n > 11) - (n > 12) - 4 * (n > 19))
                elif on["fc"]:
                    first = 2 * (n - 25)
                    for piece in range(first, min(first + 2, 7)):
                        fc(c - 3, 1 - q, piece)

            def recur(l, c, k, q):
                if k == 0 and isinstance(c, int) and c == 0:
                    return
                w = (whh0_p, whh1_p)[l]
                pq, pk = (q, k - 1) if k else (1 - q, C - 1)
                cols = slice(pk * B, (pk + 1) * B)
                z = [pre[l][q][:, m * TT + k * B:m * TT + (k + 1) * B] for m in range(MH)]
                pe.wait_ge(s_hi[l], c * C + k)
                for p in range(2):
                    for m in range(MH):
                        for kk in range(KH):
                            shared(z[m], w[:, p, kk * H + m * P:kk * H + (m + 1) * P], h_hi[l][:, pq, kk, cols])
                pe.wait_ge(s_lo[l], c * C + k)
                for m in range(MH):
                    for kk in range(KH):
                        last = shared(z[m], w[:, 0, kk * H + m * P:kk * H + (m + 1) * P],
                                      h_lo[l][:, pq, kk, cols])
                last.then_inc(s_mm[l], 1)

            def chunk(c, q, on):
                if on["in1"] and not on["rec0"]:
                    pe.wait_ge(s_hi[0], S)
                    pe.wait_ge(s_lo[0], S)
                if on["fc"] and not on["rec1"]:
                    pe.wait_ge(s_hi[1], S)
                    pe.wait_ge(s_lo[1], S)
                for k in range(C):
                    if on["rec0"]:
                        recur(0, c, k, q)
                    if k:
                        side(2 * k - 1, c, q, on)
                    if on["rec1"]:
                        recur(1, c - 2, k, q)
                    side(2 * k, c, q, on)

            pe.wait_ge(s_pool, N_POOL_SETUP)
            pe.wait_ge(s_split, 1)
            pe.wait_ge(s_rows, 16 * 8)
            pe.wait_ge(s_x1, GROUPS)
            for piece in range(4):
                in0(0, 0, piece)
            run_chunks(pe, chunk)

            pe.wait_ge(s_cum, 1)
            mm(p_tr[:, 0:1], cums[:, 1, :], first_p[:, :], start=True, stop=True).then_inc(s_cumT, 1)
            pe.wait_ge(s_past, 1)
            pe.wait_ge(s_pool, N_POOL_SETUP + NB)
            mm(p_sc[:, 0:NWIN], ones_f[:, :], past, start=True, stop=True).then_inc(s_leafp, 1)

            def flip(w, b, uses):
                pe.wait_ge(s_xs[b], uses * 16 + 16)
                if not (isinstance(w, int) and w < 2):
                    pe.wait_ge(s_xtc, w - 1)
                pe.sem_inc(s_passed, 1)
                nc.tensor.transpose(p_xT[b % 2][:, 0:P], xs[b][:, XP:PW].bitcast(F16), ident_h[:, :]).then_inc(s_xt, 1)

            def pair(w, b, uses):
                if not is_known(w, NPAIR - 1):
                    flip(w + 1, (b + 1) % NB, uses + (b + 1) // NB)
                pe.wait_ge(s_xtc, w + 1)
                pe.wait_ge(s_wl[b], uses * 32 + 32)
                if not (isinstance(w, int) and w < 2):
                    pe.wait_ge(s_prod, w - 1)
                for part, rows, x_part in ((0, WROWS, 0), (1, WROWS, 0), (0, CH, 1)):
                    for h in range(2):
                        z = p_y[b % 2][h * WIN:(h + 1) * WIN, :].rearrange("p (l o) -> p l o", l=LEVELS)
                        last = mm(z, xsT[b][0:rows, x_part, h * WIN:(h + 1) * WIN], wl[b][h][0:rows, :, part, :],
                                  start=(part == 0 and x_part == 0), stop=(x_part == 1))
                last.then_inc(s_y, 1)

            flip(0, 0, 0)
            run_pairs(pe, pair)


def kernel(x, L0_tok_w_real, L0_tok_w_imag, L0_tok_phases, L0_attn_W_ih_0, L0_attn_W_hh_0,
           L0_attn_b_ih_0, L0_attn_b_hh_0, L0_attn_W_ih_1, L0_attn_W_hh_1, L0_attn_b_ih_1,
           L0_attn_b_hh_1, L0_attn_fc_w, L0_attn_fc_b, L0_ffn_w1s, L0_ffn_b1s, L0_ffn_w2s, L0_ffn_b2s):
    import numpy as np
    import concourse.bacc as bacc
    from concourse.bass_utils import run_bass_kernel_spmd

    def taps(w):
        return np.asarray(w).transpose(2, 1, 0).reshape(K // 2, 2, CH, CH).transpose(1, 2, 0, 3).reshape(P, K // 2, CH)

    laid_out = {
        "xT": np.asarray(x).transpose(2, 1, 0).reshape(CH, SIN * B),
        "w_real": taps(L0_tok_w_real),
        "w_imag": taps(L0_tok_w_imag),
        "phases": np.asarray(L0_tok_phases).reshape(K // 2, 2).T,
        "wih0": np.asarray(L0_attn_W_ih_0).T,
        "whh0": np.asarray(L0_attn_W_hh_0).T,
        "bih0": np.asarray(L0_attn_b_ih_0).reshape(1, H),
        "bhh0": np.asarray(L0_attn_b_hh_0).reshape(1, H),
        "wih1": np.asarray(L0_attn_W_ih_1).T,
        "whh1": np.asarray(L0_attn_W_hh_1).T,
        "bih1": np.asarray(L0_attn_b_ih_1).reshape(1, H),
        "bhh1": np.asarray(L0_attn_b_hh_1).reshape(1, H),
        "fcw": np.asarray(L0_attn_fc_w).T,
        "fcb": np.asarray(L0_attn_fc_b).reshape(1, CH),
        "w1": np.asarray(L0_ffn_w1s).T,
        "b1": np.asarray(L0_ffn_b1s).reshape(1, NODES),
        "w2": np.asarray(L0_ffn_w2s),
        "b2": np.asarray(L0_ffn_b2s),
    }
    nc = bacc.Bacc("TRN2", target_bir_lowering=False, num_devices=1)
    arrays, args = {}, []
    for name, a in laid_out.items():
        a = np.ascontiguousarray(a)
        arrays[name + "_dram"] = a
        args.append(nc.dram_tensor(name + "_dram", a.shape, mybir.dt.from_np(a.dtype), kind="ExternalInput").ap())
    args.append(nc.dram_tensor("out_dram", (NT, CH), F32, kind="ExternalOutput").ap())
    tower(nc, *args)
    r = run_bass_kernel_spmd(nc, [arrays], core_ids=[0])
    got = r.results[0]["out_dram"]
    return got.reshape(S, B, CH).transpose(1, 0, 2)
```
